# Optimizing a Trainium2 kernel written in Bass

```python
import numpy as np
import jax
import jax.numpy as jnp

def _softmax(x, axis=-1):
    return jax.nn.softmax(x, axis=axis)

def _gelu(x):
    return jax.nn.gelu(x, approximate=True)

def _silu(x):
    return jax.nn.silu(x)

def _sigmoid(x):
    return jax.nn.sigmoid(x)

def _layernorm(x, axis=-1, eps=1e-05):
    m = jnp.mean(x, axis=axis, keepdims=True)
    v = jnp.var(x, axis=axis, keepdims=True)
    return (x - m) / jnp.sqrt(v + eps)

def _scatter_add(tgt, idx, src, axis=0):
    return tgt.at[idx].add(src)

def _segment_sum(src, seg, n):
    return jax.ops.segment_sum(src, seg, n)
kernel_name = 'mk_xattn_ffn_d1_seqx_r8_b61e9e'

def setup_inputs(seed: int=0):
    np.random.seed(seed)
    _w = jnp.asarray

    def _rec_inputs():
        import jax
        import jax.numpy as jnp
        _rk = jax.random.key(seed)
        x = -0.0002928 + 1 * jax.random.normal(jax.random.fold_in(_rk, 1), (64, 128, 128), jnp.float32)
        _lenS = 128 - jax.random.randint(jax.random.fold_in(_rk, 7), (64,), 0, max(1, 128 // 4) + 1, jnp.int32)
        _lenS2 = 120 - jax.random.randint(jax.random.fold_in(_rk, 8), (64,), 0, max(1, 120 // 4) + 1, jnp.int32)
        _ctx_1024P = jax.random.normal(jax.random.fold_in(_rk, 11), (64, 16, 128), jnp.float32)
        _ctx_1024c = jax.random.dirichlet(jax.random.fold_in(_rk, 511), 0.3 * jnp.ones((16,), jnp.float32), (64, 120))
        _ctx_1024t = jnp.einsum('bsk,bkd->bsd', _ctx_1024c, _ctx_1024P)
        _ctx_1024t = _ctx_1024t * jax.lax.rsqrt(jnp.mean(jnp.square(_ctx_1024t)) + 1e-12) * 0.953939
        ctx_1024 = -1.39393e-06 + 0.999914 * (_ctx_1024t + 0.3 * jax.random.normal(jax.random.fold_in(_rk, 611), (64, 120, 128), jnp.float32))
        return (x, ctx_1024)
    x, ctx_1024 = _rec_inputs()

    def _L0_xattn_setup():
        import jax, jax.numpy as jnp
        import numpy as np
        D_MODEL = 128
        HEAD = 16
        D_K = D_MODEL // HEAD
        key = jax.random.key(seed)
        ks = jax.random.split(key, 11)
        B, S = (2, 256)
        scale = 1.0 / np.sqrt(D_MODEL)
        inp = {'q': jax.random.normal(ks[0], (B, S, D_MODEL), dtype=jnp.float32), 'k': jax.random.normal(ks[1], (B, S, D_MODEL), dtype=jnp.float32), 'v': jax.random.normal(ks[2], (B, S, D_MODEL), dtype=jnp.float32), 'wq': jax.random.normal(ks[3], (D_MODEL, D_MODEL), dtype=jnp.float32) * scale, 'bq': jnp.zeros((D_MODEL,), dtype=jnp.float32), 'wk': jax.random.normal(ks[4], (D_MODEL, D_MODEL), dtype=jnp.float32) * scale, 'bk': jnp.zeros((D_MODEL,), dtype=jnp.float32), 'wv': jax.random.normal(ks[5], (D_MODEL, D_MODEL), dtype=jnp.float32) * scale, 'bv': jnp.zeros((D_MODEL,), dtype=jnp.float32), 'wo': jax.random.normal(ks[6], (D_MODEL, D_MODEL), dtype=jnp.float32) * scale, 'bo': jnp.zeros((D_MODEL,), dtype=jnp.float32)}
        return inp
    _L0_xattn_all = _L0_xattn_setup()
    _L0_xattn_in = {k: v for k, v in _L0_xattn_all.items() if k in ('wq', 'bq', 'wk', 'bk', 'wv', 'bv', 'wo', 'bo')}
    del _L0_xattn_all

    def _L0_ffn_setup():
        import jax, jax.numpy as jnp
        import numpy as np
        TOP_K = 2
        NUM_EXPERTS = 8
        DIM = 128
        HIDDEN = 352
        BS, SLEN = (2, 128)

        def _grouped_ffn(x, w1, w2, w3, counts):
            num_experts = w1.shape[0]
            ends = jnp.cumsum(counts)
            starts = ends - counts
            t = jnp.arange(x.shape[0])
            out = jnp.zeros((x.shape[0], w2.shape[-1]), x.dtype)
            for e in range(num_experts):
                m = ((t >= starts[e]) & (t < ends[e])).astype(x.dtype)[:, None]
                xe = x * m
                h = jax.nn.silu(xe @ w1[e]) * (xe @ w3[e])
                out = out + h @ w2[e] * m
            return out
        key = jax.random.key(seed)
        k = jax.random.split(key, 5)
        std = 0.02
        return {'x': jax.random.normal(k[0], (BS, SLEN, DIM), jnp.float32), 'gate_w': jax.random.normal(k[1], (NUM_EXPERTS, DIM), jnp.float32) * std, 'expert_bias': jnp.zeros((NUM_EXPERTS,), jnp.float32), 'w1': jax.random.normal(k[2], (NUM_EXPERTS, DIM, HIDDEN), jnp.float32) * std, 'w2': jax.random.normal(k[3], (NUM_EXPERTS, HIDDEN, DIM), jnp.float32) * std, 'w3': jax.random.normal(k[4], (NUM_EXPERTS, DIM, HIDDEN), jnp.float32) * std}
    _L0_ffn_all = _L0_ffn_setup()
    _L0_ffn_in = {k: v for k, v in _L0_ffn_all.items() if k in ('gate_w', 'expert_bias', 'w1', 'w2', 'w3')}
    del _L0_ffn_all
    return {'x': x, 'ctx_1024': ctx_1024, 'L0_xattn_wq': _L0_xattn_in['wq'], 'L0_xattn_bq': _L0_xattn_in['bq'], 'L0_xattn_wk': _L0_xattn_in['wk'], 'L0_xattn_bk': _L0_xattn_in['bk'], 'L0_xattn_wv': _L0_xattn_in['wv'], 'L0_xattn_bv': _L0_xattn_in['bv'], 'L0_xattn_wo': _L0_xattn_in['wo'], 'L0_xattn_bo': _L0_xattn_in['bo'], 'L0_ffn_gate_w': _L0_ffn_in['gate_w'], 'L0_ffn_expert_bias': _L0_ffn_in['expert_bias'], 'L0_ffn_w1': _L0_ffn_in['w1'], 'L0_ffn_w2': _L0_ffn_in['w2'], 'L0_ffn_w3': _L0_ffn_in['w3']}

def reference(x, ctx_1024, L0_xattn_wq, L0_xattn_bq, L0_xattn_wk, L0_xattn_bk, L0_xattn_wv, L0_xattn_bv, L0_xattn_wo, L0_xattn_bo, L0_ffn_gate_w, L0_ffn_expert_bias, L0_ffn_w1, L0_ffn_w2, L0_ffn_w3):
    import jax
    import jax.numpy as jnp

    def _L0_xattn_ref(q, k, v, wq, bq, wk, bk, wv, bv, wo, bo):
        import jax, jax.numpy as jnp
        import numpy as np
        D_MODEL = 128
        HEAD = 16
        D_K = D_MODEL // HEAD
        B, S, _ = q.shape

        def proj(x, w, b):
            y = x @ w.T + b
            return y.reshape(B, -1, HEAD, D_K).transpose(0, 2, 1, 3)
        qh, kh, vh = (proj(q, wq, bq), proj(k, wk, bk), proj(v, wv, bv))
        scores = jnp.einsum('bhqd,bhkd->bhqk', qh, kh) / jnp.sqrt(jnp.float32(D_K))
        probs = jax.nn.softmax(scores, axis=-1)
        ctx = jnp.einsum('bhqk,bhkd->bhqd', probs, vh)
        concat = ctx.transpose(0, 2, 1, 3).reshape(B, S, D_MODEL)
        return concat @ wo.T + bo

    def _L0_ffn_ref(x, gate_w, expert_bias, w1, w2, w3):
        import jax, jax.numpy as jnp
        import numpy as np
        TOP_K = 2
        NUM_EXPERTS = 8
        DIM = 128
        HIDDEN = 352
        BS, SLEN = (2, 128)

        def _grouped_ffn(x, w1, w2, w3, counts):
            num_experts = w1.shape[0]
            ends = jnp.cumsum(counts)
            starts = ends - counts
            t = jnp.arange(x.shape[0])
            out = jnp.zeros((x.shape[0], w2.shape[-1]), x.dtype)
            for e in range(num_experts):
                m = ((t >= starts[e]) & (t < ends[e])).astype(x.dtype)[:, None]
                xe = x * m
                h = jax.nn.silu(xe @ w1[e]) * (xe @ w3[e])
                out = out + h @ w2[e] * m
            return out
        bs, slen, dim = x.shape
        num_experts = gate_w.shape[0]
        xf = x.reshape(bs * slen, dim)
        scores = jax.nn.softmax((xf @ gate_w.T).astype(jnp.float32), axis=-1)
        _, sel = jax.lax.top_k(scores + expert_bias, TOP_K)
        top_scores = jnp.take_along_axis(scores, sel, axis=1).reshape(-1)
        sel_flat = sel.reshape(-1)
        counts = jnp.zeros((num_experts,), jnp.int32).at[sel_flat].add(1)
        order = jnp.argsort(sel_flat, stable=True)
        top_scores_sorted = top_scores[order]
        token_idx = order // TOP_K
        routed = xf[token_idx] * top_scores_sorted[:, None].astype(xf.dtype)
        routed_out = _grouped_ffn(routed, w1, w2, w3, counts)
        out = jnp.zeros_like(xf).at[token_idx].add(routed_out)
        return out.reshape(bs, slen, dim)
    x = x + _L0_xattn_ref(_layernorm(x, axis=-1), ctx_1024, ctx_1024, L0_xattn_wq, L0_xattn_bq, L0_xattn_wk, L0_xattn_bk, L0_xattn_wv, L0_xattn_bv, L0_xattn_wo, L0_xattn_bo)
    x = x + _L0_ffn_ref(_layernorm(x, axis=-1), L0_ffn_gate_w, L0_ffn_expert_bias, L0_ffn_w1, L0_ffn_w2, L0_ffn_w3)
    return x

_drawn_inputs = setup_inputs


def setup_inputs(seed=0):
    import zlib

    import numpy as np

    out = dict(_drawn_inputs(seed))
    spreads = {'L0_xattn_bq': (0.0, 0.374),
     'L0_xattn_bk': (0.0, 0.8),
     'L0_xattn_bv': (0.0, 0.1),
     'L0_xattn_bo': (0.0, 0.1),
     'L0_ffn_expert_bias': (0.0, 0.8)}
    factors = {'L0_ffn_gate_w': 8.0, 'L0_ffn_w1': 8.0, 'L0_ffn_w2': 8.0, 'L0_ffn_w3': 8.0}
    for name, (base, spread) in spreads.items():
        noise = np.random.default_rng([zlib.crc32(name.encode()), seed]).standard_normal(out[name].shape)
        drawn = base * np.exp(spread * noise) if base else spread * noise
        out[name] = jnp.asarray(drawn.astype(out[name].dtype))
    for name, factor in factors.items():
        out[name] = (out[name] * factor).astype(out[name].dtype)
    return out
```

```python
from contextlib import ExitStack

import concourse.bass as bass
from concourse import mybir

F32 = mybir.dt.float32
BF16 = mybir.dt.bfloat16
I32 = mybir.dt.int32
U32 = mybir.dt.uint32
ALU = mybir.AluOpType
ACT = mybir.ActivationFunctionType
AX = mybir.AxisListType

P = 128
HEADS = 16
EPS = 1e-5


class Counter:

    def __init__(self, sem, step=1):
        self.sem, self.step = sem, step

    def done(self, ins):
        ins.then_inc(self.sem, self.step)

    def wait(self, eng, runs):
        if isinstance(runs, int) and runs <= 0:
            return
        eng.wait_ge(self.sem, runs * self.step)


class Ring(Counter):

    def __init__(self, sem, n, per=1):
        super().__init__(sem, 16)
        self.n, self.per = n, per

    def landed(self, eng, item, q):
        eng.wait_ge(self.sem, (item - q) * (16 * self.per // self.n) + 16 * self.per)

    def reusable(self, eng, item, q):
        if not (isinstance(item, int) and item < self.n):
            eng.wait_ge(self.sem, (item - q) * (16 * self.per // self.n))


def walk(eng, steps, per, unroll, first, last, low, high, total):

    def one(rnd, phase):
        for g in range(per):
            for slot, run in steps:
                if (slot - g) % per == 0:
                    back = (slot - g) // per
                    item = rnd - back
                    if isinstance(item, int) and not 0 <= item < total:
                        continue
                    run(item, (phase - back) % unroll)

    for r in range(first, low):
        one(r, r % unroll)
    with eng.Fori(0, (high - low) // unroll) as r:
        for u in range(unroll):
            one(r * unroll + (low + u), (low + u) % unroll)
    for r in range(high, last + 1):
        one(r, r % unroll)


def build(nc, x, ctx_in, wqT, bq, wkT, bk, wvT, bv, woT, bo, gateT, ebias, w1, w2, w3, out):
    B, S, D = x.shape
    K = ctx_in.shape[1]
    DH = D // HEADS
    E, _, HID = w1.shape
    T = B * S
    SCALE = float(DH) ** -0.5
    GROUPS = 4
    HC = (HID + P - 1) // P
    CHUNK = [min(P, HID - c * P) for c in range(HC)]
    CAP = T + P
    NT = 2 * T // P + E - 1
    SPARE = (E - 1) * P
    ROW = D + 1
    NOWHERE = 4 * T
    assert S == P and D == P and HEADS == 4 * GROUPS and DH == 8

    xs_dram = nc.dram_tensor("expert_rows", [E * CAP + SPARE, ROW], F32, kind="Internal").ap()
    y_dram = nc.dram_tensor("expert_results", [2 * T, D], F32, kind="Internal").ap()

    with ExitStack() as stack:
        def sb(name, shape, dt=F32):
            return stack.enter_context(nc.sbuf_tensor(name, shape, dt))

        def ps(name, shape, dt=F32):
            return stack.enter_context(nc.psum_tensor(name, shape, dt))

        names = iter(range(10 ** 6))

        def counter(name, step=1):
            return Counter(stack.enter_context(nc.semaphore(f"{name}_{next(names)}")), step)

        def ring(name, n, per=1):
            return Ring(stack.enter_context(nc.semaphore(name)), n, per)

        wq_s, wk_s, wv_s, wo_s = (sb(n, [P, D]) for n in ("wq_s", "wk_s", "wv_s", "wo_s"))
        gate_s = sb("gate_s", [P, E])
        bq_s, bk_s, bqs_s = sb("bq_s", [P, 1]), sb("bk_s", [P, 1]), sb("bqs_s", [P, 1])
        bv_b, bo_b, eb_b = sb("bv_b", [P, D]), sb("bo_b", [P, D]), sb("eb_b", [P, E])
        w1_s, w3_s = sb("w1_s", [P, E * HID]), sb("w3_s", [P, E * HID])
        w2_s = sb("w2_s", [P, HC, E * D])
        ident = sb("ident", [P, P])
        head1, headmask = sb("head1", [P, HEADS]), sb("headmask", [P, 4])
        before = sb("before", [P, P], BF16)
        ones = sb("ones", [P, P], BF16)
        iota_e = sb("iota_e", [P, E])
        region = sb("region", [P, E])
        minus_half = sb("minus_half", [P, 1])
        place_of = sb("place_of", [P, B, 2], I32)
        iota_p = sb("iota_p", [P, 1])
        XB = 4
        x_s, c_s = sb("x_s", [P, XB, D]), sb("c_s", [P, XB, D])
        x2 = sb("x2", [P, B, D])
        st1, mv1, ve1, rs1 = sb("st1", [P, 6]), sb("mv1", [P, 2, 2]), sb("ve1", [P, 2]), sb("rs1", [P, 2])
        st2, mv2, ve2, rs2 = sb("st2", [P, 6]), sb("mv2", [P, 2, 2]), sb("ve2", [P, 2]), sb("rs2", [P, 2])
        xn = sb("xn", [P, 2, D])
        xcT = sb("xcT", [P, D + K])
        qT, kz = sb("qT", [P, 2, P]), sb("kz", [P, 2, 4, K])
        v1 = sb("v1", [P, 4, HEADS, DH + 1])
        mx = sb("mx", [P, 2, 4])
        prob = sb("prob", [P, 2, 4, K])
        pT = sb("pT", [P, 2, 4, P])
        uT = sb("uT", [P, GROUPS, P])
        rden, on, onT = sb("rden", [P, HEADS]), sb("on", [P, D]), sb("onT", [P, P])
        x2s = sb("x2s", [P, 2, D])
        xn2, xn2T = sb("xn2", [P, 2, D]), sb("xn2T", [P, P])
        nmx, ex, esum = sb("nmx", [P, 1]), sb("ex", [P, 2, E]), sb("esum", [P, 2])
        rsum, biased = sb("rsum", [P, 2]), sb("biased", [P, E])
        top, topi, topf = sb("top", [P, 8]), sb("topi", [P, 8], U32), sb("topf", [P, 2, 2])
        sel1, sel = sb("sel1", [P, E]), sb("sel", [P, E], BF16)
        junk = sb("junk", [P, 4, E])
        gates = sb("gates", [P, 2, 2])
        carry = sb("carry", [P, 2, E])
        row_of, places = sb("row_of", [P, E]), sb("places", [P, 2])
        places_i = sb("places_i", [P, 2, 2], I32)
        rows = sb("rows", [P, 2, 2, ROW])
        cnt, cnt_i, cnt_j = sb("cnt", [P, E]), sb("cnt_i", [P, E], I32), sb("cnt_j", [P, E], I32)
        ntile, upto, jump = sb("ntile", [P, E]), sb("upto", [P, E]), sb("jump", [P, E])
        tvec, passed, first_row = sb("tvec", [1, NT]), sb("passed", [1, NT]), sb("first_row", [1, NT])
        jumps = sb("jumps", [1, NT])
        t_exp, t_row = sb("t_exp", [1, NT], I32), sb("t_row", [1, NT], I32)
        pad_f, pad_i = sb("pad_f", [P, E]), sb("pad_i", [P, E], I32)
        padding = sb("padding", [P, ROW])
        xs = sb("xs", [P, 4, ROW])
        where = sb("where", [P, 4], I32)
        xsT = sb("xsT", [P, 2, P])
        act, hid = sb("act", [P, 2, HID]), sb("hid", [P, 2, HID])
        hidT = sb("hidT", [P, 2, HC, P])
        y_s = sb("y_s", [P, 4, D])
        LG = 4
        ya, yb, tot = sb("ya", [P, 2, LG, D]), sb("yb", [P, 2, LG, D]), sb("tot", [P, 2, LG, D])

        bank = [ps(f"bank{n}", [P, 512]) for n in range(8)]
        score_b, prT_b, u_b, m_a, m_b, m_c = bank[0:2], bank[2:4], bank[4], bank[5], bank[6], bank[7]
        h1_b, h3_b, hT_b, y_b, xT_b = bank[0:2], bank[2:4], bank[4:6], bank[6], bank[7]

        weights, ffn_weights, consts = counter("weights", 16), counter("ffn_weights", 16), counter("consts")
        mask_r, ready = counter("mask_r"), counter("ready")
        spare_r = counter("spare_r", 16)
        c = {n: counter(n) for n in (
            "stats1 var1 eps1 rstd1 xn xbo ln1T ln1T_e proj qT kz v S max sub exp PT PT_e PV U OT rden on onT "
            "onT_e O x2 keep stats2 var2 eps2 rstd2 xn2 xn2T xn2T_e logits nmx ex rsum biased top topi topf sel1 sel "
            "gate1 gate2 pos row_of carry place1 place2 places_i rows1 rows2 placed1 placed2").split()}
        loads = [ring(f"loads{n}", XB, 2) for n in range(XB)]
        scat = [ring(f"scat{n}", 2, 2) for n in range(2)]
        table, padded, pad_rows = counter("table"), counter("padded", 16), counter("pad_rows")
        f = {n: counter("f_" + n) for n in "xT xT_e where h act hid hT hT_e y y_e".split()}
        tile_in = [ring(f"tile_in{n}", 4) for n in range(4)]
        tile_out = [ring(f"tile_out{n}", 4) for n in range(4)]
        y_in = [ring(f"y_in{n}", 2, 2) for n in range(2)]
        added, total, stored = counter("added"), counter("total"), [ring(f"stored{n}", 2) for n in range(2)]
        block = stack.enter_context(nc.Block())

        N_WEIGHTS, N_FFN, N_CONSTS = 10, 2 + HC, 18

        def batches(eng, steps):
            walk(eng, steps, GROUPS, 4, -2, B + 2, 6, B - 2, B)

        def tiles(eng, steps):
            walk(eng, steps, 1, 4, -1, NT + 1, 6, 6 + (NT - 7) // 4 * 4, NT)

        def settled(eng):
            eng.nop(nofuse=True)

        def upto_b(n):
            return min(n, B) if isinstance(n, int) else n

        @block.sync
        def _(eng):
            for dst, src in ((wq_s, wqT), (wk_s, wkT), (wv_s, wvT), (wo_s, woT), (gate_s, gateT)):
                weights.done(eng.dma_start(dst[:, :], src))
            for dst, src in ((bq_s, bq), (bk_s, bk)):
                weights.done(eng.dma_start(dst[:, :], src.rearrange("(p a) -> p a", a=1)))
            for dst, src in ((bv_b, bv), (bo_b, bo), (eb_b, ebias)):
                n = src.shape[0]
                weights.done(eng.dma_start(dst[:, :], src.rearrange("(a n) -> a n", a=1).broadcast_to((P, n))))

            def load(b, q):
                for step in ("xn", "xbo", "ln1T"):
                    c[step].wait(eng, b - XB + 1)
                loads[q].done(eng.dma_start(x_s[:, q, :], x[bass.ds(b, 1), :, :].rearrange("a s d -> (a s) d")))
                loads[q].done(eng.dma_start(c_s[0:K, q, :],
                                            ctx_in[bass.ds(b, 1), :, :].rearrange("a s d -> (a s) d")))

            for b in range(XB):
                load(b, b)
            for dst, src in ((w1_s, w1), (w3_s, w3)):
                ffn_weights.done(eng.dma_start(dst[:, :].rearrange("p (e h) -> p e h", e=E),
                                               src.rearrange("e p h -> p e h")))
            for h in range(HC):
                ffn_weights.done(eng.dma_start(
                    w2_s[0:CHUNK[h], h, :].rearrange("p (e n) -> p e n", e=E),
                    w2[:, h * P:h * P + CHUNK[h], :].rearrange("e p n -> p e n")))
            pad_rows.wait(eng, 2)
            for n in range(E - 1):
                r = E * CAP + n * P
                spare_r.done(eng.dma_start(xs_dram[r:r + P, :], padding[:, :]))
            with eng.Fori(1, B // XB) as r:
                for q in range(XB):
                    load(r * XB + q, q)

            for n in range(2):
                scat[n].wait(eng, B)
            padded.wait(eng, E)
            spare_r.wait(eng, E - 1)
            table.wait(eng, 1)

            def tile_load(t, q):
                f["xT"].wait(eng, t - 3)
                f["where"].wait(eng, t - 3)
                row = eng.value_load(t_row[0:1, bass.ds(t, 1)], min_val=0, max_val=E * CAP + SPARE - P)
                tile_in[q].done(eng.dma_start(xs[:, q, :], xs_dram[bass.ds(row, P), :]))

            for t in range(4):
                tile_load(t, t)
            last = NT // 4 * 4
            with eng.Fori(1, last // 4) as r:
                for q in range(4):
                    tile_load(r * 4 + q, q)
            for t in range(last, NT):
                tile_load(t, t % 4)

            for q in range(4):
                tile_out[q].wait(eng, (NT - q + 3) // 4)

            def y_load(n, q):
                added.wait(eng, n - 1)
                for dst, base in ((ya, 0), (yb, T)):
                    src = y_dram[bass.ds(n * (LG * P) + base, LG * P), :].rearrange("(t p) d -> p t d", p=P)
                    y_in[q].done(eng.dma_start(dst[:, q, :, :], src))

            for n in range(2):
                y_load(n, n)
            with eng.Fori(1, B // LG // 2) as r:
                for q in range(2):
                    y_load(r * 2 + q, q)

        @block.gpsimd
        def _(eng):
            pad_rows.done(eng.memset(padding[:, 0:D], 0.0))
            pad_rows.done(eng.memset(padding[:, D:ROW].bitcast(I32), NOWHERE))
            made = [0]

            def const(ins):
                consts.done(ins)
                made[0] += 1
                consts.wait(eng, made[0])

            const(eng.memset(minus_half[:, :], -0.5))
            const(eng.memset(ident[:, :], 0.0))
            const(eng.affine_select(out=ident[:, :], in_=ident[:, :], compare_op=ALU.not_equal, fill=1.0,
                                    base=0, pattern=[[-1, P]], channel_multiplier=1))
            const(eng.memset(head1[:, :], 1.0))
            const(eng.affine_select(out=head1[:, :], in_=head1[:, :], compare_op=ALU.is_ge, fill=0.0,
                                    base=0, pattern=[[-DH, HEADS]], channel_multiplier=1))
            const(eng.affine_select(out=head1[:, :], in_=head1[:, :], compare_op=ALU.is_ge, fill=0.0,
                                    base=DH - 1, pattern=[[DH, HEADS]], channel_multiplier=-1))
            const(eng.memset(before[:, :], 1.0))
            const(eng.affine_select(out=before[:, :], in_=before[:, :], compare_op=ALU.is_gt, fill=0.0,
                                    base=0, pattern=[[1, P]], channel_multiplier=-1))
            const(eng.memset(ones[:, :], 1.0))
            const(eng.iota(iota_e[:, :], [[1, E]], base=0, channel_multiplier=0,
                           allow_small_or_imprecise_dtypes=True))
            const(eng.iota(region[:, :], [[CAP, E]], base=0, channel_multiplier=0,
                           allow_small_or_imprecise_dtypes=True))
            const(eng.iota(carry[:, 0, :], [[CAP, E]], base=0, channel_multiplier=0,
                           allow_small_or_imprecise_dtypes=True))
            const(eng.iota(place_of[:, :, :], [[P, B], [T, 2]], base=0, channel_multiplier=1))
            const(eng.iota(iota_p[:, :], [[0, 1]], base=0, channel_multiplier=1,
                           allow_small_or_imprecise_dtypes=True))
            const(eng.iota(tvec[:, :], [[1, NT]], base=0, channel_multiplier=0,
                           allow_small_or_imprecise_dtypes=True))
            const(eng.memset(v1[:, :, :, :], 1.0))
            const(eng.memset(hidT[:, :, :, :], 0.0))
            const(eng.memset(xcT[:, :], 0.0))
            assert made[0] == N_CONSTS
            weights.wait(eng, N_WEIGHTS)

            def norm1(b, q):
                h = q % 2
                c["var1"].wait(eng, b + 1)
                c["xn"].wait(eng, b - 1)
                settled(eng)
                c["eps1"].done(eng.tensor_scalar(ve1[:, h:h + 1], mv1[:, h, 1:2], EPS, None, ALU.add))
                c["eps1"].wait(eng, b + 1)
                c["rstd1"].done(eng.tensor_tensor(rs1[:, h:h + 1], ve1[:, h:h + 1], minus_half[:, :], ALU.pow))
                c["rstd1"].wait(eng, b + 1)
                c["ln1T"].wait(eng, b - 1)
                settled(eng)
                c["xn"].done(eng.tensor_scalar(xn[:, h, :], x_s[:, q, :], mv1[:, h, 0:1], rs1[:, h:h + 1],
                                               ALU.subtract, ALU.mult))
                c["xbo"].done(eng.tensor_tensor(x2[:, bass.ds(b, 1), :].rearrange("p a d -> p (a d)"),
                                                x_s[:, q, :], bo_b[:, :], ALU.add))

            def norm2(b, q):
                h = q % 2
                c["var2"].wait(eng, b + 1)
                c["xn2"].wait(eng, b - 1)
                settled(eng)
                c["eps2"].done(eng.tensor_scalar(ve2[:, h:h + 1], mv2[:, h, 1:2], EPS, None, ALU.add))
                c["eps2"].wait(eng, b + 1)
                c["rstd2"].done(eng.tensor_tensor(rs2[:, h:h + 1], ve2[:, h:h + 1], minus_half[:, :], ALU.pow))
                c["rstd2"].wait(eng, b + 1)
                c["xn2T"].wait(eng, b - 1)
                c["rows2"].wait(eng, b - 1)
                settled(eng)
                c["xn2"].done(eng.tensor_scalar(xn2[:, h, :], x2s[:, h, :],
                                                mv2[:, h, 0:1], rs2[:, h:h + 1], ALU.subtract, ALU.mult))
                c["keep"].done(eng.tensor_copy(x2[:, bass.ds(b, 1), :].rearrange("p a d -> p (a d)"),
                                               x2s[:, h, :]))

            def scatter(b, q):
                h = q % 2
                scat[h].reusable(eng, b, h)
                c["gate1"].wait(eng, b + 1)
                c["gate2"].wait(eng, b + 1)
                c["xn2"].wait(eng, b + 1)
                settled(eng)
                for k in range(2):
                    c[f"rows{k + 1}"].done(eng.tensor_scalar(rows[:, h, k, 0:D], xn2[:, h, :],
                                                             gates[:, h, k:k + 1], rsum[:, h:h + 1],
                                                             ALU.mult, ALU.mult))
                c["placed1"].done(eng.tensor_copy(
                    rows[:, h, :, D:ROW].bitcast(I32),
                    place_of[:, bass.ds(b, 1), :].rearrange("p a k -> p k a")))
                c["rows2"].wait(eng, b + 1)
                c["placed1"].wait(eng, b + 1)
                c["places_i"].wait(eng, b + 1)
                settled(eng)
                for k in range(2):
                    scat[h].done(eng.indirect_dma_start(
                        xs_dram, bass.IndirectOffsetOnAxis(ap=places_i[:, h, k:k + 1], axis=0),
                        rows[:, h, k, :], None))

            batches(eng, [(8, norm2), (13, scatter), (-8, norm1)])

            table.wait(eng, 1)
            for e in range(E):
                padded.done(eng.indirect_dma_start(
                    xs_dram, bass.IndirectOffsetOnAxis(ap=pad_i[:, e:e + 1], axis=0), padding[:, :], None))

            def places(t, q):
                tile_in[q].landed(eng, t, q)
                tile_out[q].reusable(eng, t, q)
                settled(eng)
                f["where"].done(eng.tensor_copy(where[:, q:q + 1], xs[:, q, D:ROW].bitcast(I32)))

            def results(t, q):
                f["y_e"].wait(eng, t + 1)
                f["where"].wait(eng, t + 1)
                settled(eng)
                tile_out[q].done(eng.indirect_dma_start(
                    y_dram, bass.IndirectOffsetOnAxis(ap=where[:, q:q + 1], axis=0), y_s[:, q, :], None,
                    bounds_check=2 * T - 1, oob_is_err=False))

            tiles(eng, [(-1, places), (2, results)])

        @block.vector
        def _(eng):
            consts.wait(eng, N_CONSTS)
            weights.wait(eng, N_WEIGHTS)
            mask_r.done(eng.tensor_reduce(headmask[:, :], head1[:, :].rearrange("p (g j) -> p j g", j=4),
                                          AX.X, ALU.add))
            mask_r.wait(eng, 1)
            ready.done(eng.tensor_scalar(bqs_s[:, :], bq_s[:, :], SCALE, None, ALU.mult))
            ready.done(eng.memset(u_b[:, :], 0.0))

            def stats1(b, q):
                h = q % 2
                loads[q].landed(eng, b, q)
                c["var1"].wait(eng, b)
                settled(eng)
                c["stats1"].done(eng.bn_stats(st1[:, :], x_s[:, q, :]))
                c["stats1"].wait(eng, b + 1)
                c["xn"].wait(eng, b - 1)
                settled(eng)
                c["var1"].done(eng.bn_aggr(mv1[:, h, :], st1[:, :]))

            def keys(b, q):
                h = q % 2
                c["proj"].wait(eng, b + 1)
                c["S"].wait(eng, 4 * b - 4)
                c["kz"].done(eng.scalar_tensor_tensor(
                    out=kz[:, h, :, :], in0=m_b[:, 0:K].unsqueeze(1).broadcast_to((P, 4, K)),
                    scalar=bk_s[:, 0:1], in1=headmask[:, :].unsqueeze(2).broadcast_to((P, 4, K)),
                    op0=ALU.add, op1=ALU.mult))
                c["PV"].wait(eng, 4 * b - 12)
                c["v"].done(eng.tensor_tensor(
                    v1[0:K, q, :, 0:DH], m_b[0:K, P:2 * P].rearrange("p (n d) -> p n d", d=DH),
                    bv_b[0:K, :].rearrange("p (n d) -> p n d", d=DH), ALU.add))

            def softmax(g):
                def run(b, q):
                    n, h = 4 * b + g, g % 2
                    s = score_b[h][:, 0:4 * K].rearrange("p (j k) -> p j k", j=4)
                    c["S"].wait(eng, n + 1)
                    c["sub"].wait(eng, n - 1)
                    c["max"].done(eng.tensor_reduce(mx[:, h, :], s, AX.X, ALU.max))
                    c["max"].wait(eng, n + 1)
                    c["PT"].wait(eng, n - 1)
                    c["sub"].done(eng.tensor_tensor(prob[:, h, :, :], s,
                                                    mx[:, h, :].unsqueeze(2).broadcast_to((P, 4, K)),
                                                    ALU.subtract))
                return run

            def divide(b, q):
                o = m_b[:, :].rearrange("p (n w) -> p n w", w=32)
                c["OT"].wait(eng, b + 1)
                c["on"].wait(eng, b)
                c["rden"].done(eng.reciprocal(rden[:, :].unsqueeze(2), o[:, :, DH:DH + 1]))
                c["rden"].wait(eng, b + 1)
                c["onT"].wait(eng, b)
                c["on"].done(eng.tensor_tensor(on[:, :].rearrange("p (n d) -> p n d", d=DH), o[:, :, 0:DH],
                                               rden[:, :].unsqueeze(2).broadcast_to((P, HEADS, DH)), ALU.mult))

            def residual(b, q):
                h = q % 2
                c["O"].wait(eng, b + 1)
                c["xbo"].wait(eng, b + 1)
                c["keep"].wait(eng, b - 1)
                c["x2"].done(eng.tensor_tensor(x2s[:, h, :], m_c[:, 0:D],
                                               x2[:, bass.ds(b, 1), :].rearrange("p a d -> p (a d)"), ALU.add))
                c["x2"].wait(eng, b + 1)
                c["var2"].wait(eng, b)
                settled(eng)
                c["stats2"].done(eng.bn_stats(st2[:, :], x2s[:, h, :]))
                c["stats2"].wait(eng, b + 1)
                c["xn2"].wait(eng, b - 1)
                settled(eng)
                c["var2"].done(eng.bn_aggr(mv2[:, h, :], st2[:, :]))

            def logit_max(b, q):
                c["logits"].wait(eng, b + 1)
                c["ex"].wait(eng, b)
                c["nmx"].done(eng.tensor_reduce(nmx[:, :], m_a[:, 0:E], AX.X, ALU.max, negate=True))

            def choose(b, q):
                h = q % 2
                c["ex"].wait(eng, b + 1)
                c["rows2"].wait(eng, b - 1)
                c["rsum"].done(eng.reciprocal(rsum[:, h:h + 1], esum[:, h:h + 1]))
                c["rsum"].wait(eng, b + 1)
                c["topi"].wait(eng, b)
                c["biased"].done(eng.scalar_tensor_tensor(out=biased[:, :], in0=ex[:, h, :],
                                                          scalar=rsum[:, h:h + 1], in1=eb_b[:, :],
                                                          op0=ALU.mult, op1=ALU.add))
                c["biased"].wait(eng, b + 1)
                settled(eng)
                c["top"].done(eng.max(top[:, :], biased[:, :]))
                c["top"].wait(eng, b + 1)
                c["topf"].wait(eng, b)
                settled(eng)
                c["topi"].done(eng.max_index(topi[:, :], top[:, :], biased[:, :]))
                c["topi"].wait(eng, b + 1)
                c["place2"].wait(eng, b - 1)
                c["topf"].done(eng.tensor_copy(topf[:, h, :], topi[:, 0:2]))
                c["topf"].wait(eng, b + 1)
                c["sel"].wait(eng, b)
                c["sel1"].done(eng.tensor_scalar(sel1[:, :], iota_e[:, :], topf[:, h, 0:1], None, ALU.is_equal))
                c["sel1"].wait(eng, b + 1)
                c["pos"].wait(eng, b)
                c["sel"].done(eng.scalar_tensor_tensor(out=sel[:, :], in0=iota_e[:, :],
                                                       scalar=topf[:, h, 1:2], in1=sel1[:, :],
                                                       op0=ALU.is_equal, op1=ALU.add))
                for k in range(2):
                    c[f"gate{k + 1}"].wait(eng, b)
                    c[f"gate{k + 1}"].done(eng.scalar_tensor_tensor(
                        out=junk[:, k, :], in0=iota_e[:, :], scalar=topf[:, h, k:k + 1], in1=ex[:, h, :],
                        op0=ALU.is_equal, op1=ALU.mult, accum_out=gates[:, h, k:k + 1]))

            def rank(b, q):
                h = q % 2
                c["pos"].wait(eng, b + 1)
                c["place2"].wait(eng, b)
                c["carry"].wait(eng, b)
                c["row_of"].done(eng.tensor_tensor(row_of[:, :], m_c[:, 0:E], carry[:, h, :], ALU.add))
                c["row_of"].wait(eng, b)
                c["carry"].done(eng.tensor_tensor(carry[:, 1 - h, :], m_c[:, E:2 * E], carry[:, h, :], ALU.add))
                c["row_of"].wait(eng, b + 1)
                c["places_i"].wait(eng, b)
                for k in range(2):
                    c[f"place{k + 1}"].done(eng.scalar_tensor_tensor(
                        out=junk[:, 2 + k, :], in0=iota_e[:, :], scalar=topf[:, h, k:k + 1],
                        in1=row_of[:, :], op0=ALU.is_equal, op1=ALU.mult, accum_out=places[:, k:k + 1]))
                c["place1"].wait(eng, b + 1)
                c["place2"].wait(eng, b + 1)
                scat[h].reusable(eng, b, h)
                c["places_i"].done(eng.tensor_copy(places_i[:, h, :], places[:, :]))

            batches(eng, [(g, softmax(g)) for g in range(4)] +
                    [(-4, keys), (6, divide), (8, residual), (11, logit_max), (12, choose), (13, rank),
                     (-8, stats1)])

            made = [0]

            def link(ins):
                c["row_of"].done(ins)
                made[0] += 1
                c["row_of"].wait(eng, B + made[0])

            c["carry"].wait(eng, B)
            c["keep"].wait(eng, B)
            final = carry[:, B % 2, :]
            link(eng.tensor_tensor(cnt[:, :], final, region[:, :], ALU.subtract))
            link(eng.tensor_scalar(cnt_i[:, :], cnt[:, :], float(P - 1), None, ALU.add))
            link(eng.tensor_scalar(cnt_j[:, :], cnt_i[:, :], P.bit_length() - 1, None, ALU.logical_shift_right))
            link(eng.tensor_copy(ntile[:, :], cnt_j[:, :]))
            link(eng.tensor_scalar(jump[:, :], ntile[:, :], -float(P), float(CAP), ALU.mult, ALU.add))
            link(eng.tensor_copy(upto[:, 0:1], ntile[:, 0:1]))
            for e in range(1, E):
                link(eng.tensor_tensor(upto[:, e:e + 1], upto[:, e - 1:e], ntile[:, e:e + 1], ALU.add))
            link(eng.tensor_scalar(passed[:, :], tvec[:, :], upto[0:1, 0:1], None, ALU.is_ge))
            link(eng.tensor_scalar(first_row[:, :], tvec[:, :], float(P), None, ALU.mult))
            for e in range(E):
                if e:
                    link(eng.scalar_tensor_tensor(out=passed[:, :], in0=tvec[:, :], scalar=upto[0:1, e:e + 1],
                                                  in1=passed[:, :], op0=ALU.is_ge, op1=ALU.add))
                link(eng.tensor_scalar(jumps[:, :], tvec[:, :], upto[0:1, e:e + 1], jump[0:1, e:e + 1],
                                       ALU.is_ge, ALU.mult))
                link(eng.tensor_tensor(first_row[:, :], first_row[:, :], jumps[:, :], ALU.add))
            link(eng.tensor_scalar(t_exp[:, :], passed[:, :], float(E - 1), None, ALU.min))
            link(eng.tensor_copy(t_row[:, :], first_row[:, :]))
            link(eng.tensor_scalar(pad_f[:, :], final, iota_p[:, 0:1], None, ALU.add))
            for b in hT_b:
                link(eng.memset(b[:, :], 0.0))
            table.done(eng.tensor_copy(pad_i[:, :], pad_f[:, :]))

            def gated(t, q):
                h = q % 2
                f["act"].wait(eng, t + 1)
                f["hT"].wait(eng, t - 1)
                f["hid"].done(eng.tensor_tensor(hid[:, h, :], h3_b[h][:, 0:HID], act[:, h, :], ALU.mult))

            def hidden(t, q):
                h = q % 2
                f["hT"].wait(eng, t + 1)
                f["y"].wait(eng, t - 1)
                f["hT_e"].done(eng.tensor_copy(hidT[:, h, :, :],
                                               hT_b[h][:, 0:HC * P].rearrange("p (c t) -> p c t", c=HC)))

            tiles(eng, [(0, gated), (1, hidden)])

            def add_up(n, q):
                y_in[q].landed(eng, n, q)
                stored[q].reusable(eng, n, q)
                added.done(eng.tensor_tensor(tot[:, q, :, :], ya[:, q, :, :], yb[:, q, :, :], ALU.add))
                added.wait(eng, n + 1)
                total.done(eng.tensor_tensor(tot[:, q, :, :], tot[:, q, :, :],
                                             x2[:, bass.ds(n * LG, LG), :], ALU.add))

            for n in range(2):
                add_up(n, n)
            with eng.Fori(1, B // LG // 2) as r:
                for q in range(2):
                    add_up(r * 2 + q, q)

        @block.scalar
        def _(eng):
            ready.wait(eng, 2)

            def exps(g):
                def run(b, q):
                    n, h = 4 * b + g, g % 2
                    c["sub"].wait(eng, n + 1)
                    c["exp"].done(eng.activation(prob[:, h, :, :], prob[:, h, :, :], ACT.Exp))
                return run

            def probs(g):
                def run(b, q):
                    n, h = 4 * b + g, g % 2
                    c["PT"].wait(eng, n + 1)
                    c["PV"].wait(eng, n - 1)
                    c["PT_e"].done(eng.activation(pT[0:K, h, :, :],
                                                  prT_b[h][0:K, :].rearrange("k (j t) -> k j t", j=4), ACT.Copy))
                return run

            def inputs(b, q):
                c["ln1T"].wait(eng, b + 1)
                c["proj"].wait(eng, b)
                c["ln1T_e"].done(eng.activation(xcT[:, :], m_a[:, 0:D + K], ACT.Copy))

            def queries(b, q):
                h = q % 2
                c["proj"].wait(eng, b + 1)
                c["S"].wait(eng, 4 * b - 4)
                c["qT"].done(eng.activation(qT[:, h, :], m_a[:, 0:P], ACT.Identity, bias=bqs_s[:, 0:1],
                                            scale=SCALE))

            def context(b, q):
                c["PV"].wait(eng, 4 * b + 4)
                c["OT"].wait(eng, b)
                c["U"].done(eng.activation(uT[:, :, :], u_b[:, :].rearrange("p (g t) -> p g t", g=GROUPS),
                                           ACT.Copy))

            def heads(b, q):
                c["onT"].wait(eng, b + 1)
                c["O"].wait(eng, b)
                c["onT_e"].done(eng.activation(onT[:, :], m_c[:, 0:P], ACT.Copy))

            def normed(b, q):
                c["xn2T"].wait(eng, b + 1)
                c["logits"].wait(eng, b)
                c["xn2T_e"].done(eng.activation(xn2T[:, :], m_c[:, 0:P], ACT.Copy))

            def router(b, q):
                h = q % 2
                c["nmx"].wait(eng, b + 1)
                c["gate2"].wait(eng, b - 1)
                c["ex"].done(eng.activation(ex[:, h, :], m_a[:, 0:E], ACT.Exp, bias=nmx[:, 0:1],
                                            accum_out=esum[:, h:h + 1]))

            batches(eng, [(g, exps(g)) for g in range(4)] + [(g + 1, probs(g)) for g in range(4)] +
                    [(5, context), (7, heads), (10, normed), (11, router), (-6, inputs), (-4, queries)])

            def tokens(t, q):
                h = q % 2
                f["xT"].wait(eng, t + 1)
                f["h"].wait(eng, t - 1)
                f["xT_e"].done(eng.activation(xsT[:, h, :], xT_b[:, 0:P], ACT.Copy))

            def silu(t, q):
                h = q % 2
                f["h"].wait(eng, t + 1)
                f["hid"].wait(eng, t - 1)
                f["act"].done(eng.activation(act[:, h, :], h1_b[h][:, 0:HID], ACT.Silu))

            def result(t, q):
                f["y"].wait(eng, t + 1)
                tile_out[q].reusable(eng, t, q)
                f["y_e"].done(eng.activation(y_s[:, q, :], y_b[:, 0:D], ACT.Copy))

            tiles(eng, [(-1, tokens), (0, silu), (2, result)])

            def store(n, q):
                total.wait(eng, n + 1)
                dst = out.rearrange("b s d -> s b d")[:, bass.ds(n * LG, LG), :]
                stored[q].done(eng.dma_start(dst, tot[:, q, :, :]))

            with eng.Fori(0, B // LG // 2) as r:
                for q in range(2):
                    store(r * 2 + q, q)
            for q in range(2):
                stored[q].wait(eng, B // LG // 2)

        @block.tensor
        def _(eng):
            ready.wait(eng, 2)

            def inputs(b, q):
                h = q % 2
                c["xn"].wait(eng, b + 1)
                c["qT"].wait(eng, b)
                eng.transpose(m_a[:, 0:D], xn[:, h, :], ident[:, :])
                c["ln1T"].done(eng.transpose(m_a[:, D:D + K], c_s[0:K, q, :], ident[0:K, 0:K]))

            def project(b, q):
                c["ln1T_e"].wait(eng, b + 1)
                c["ex"].wait(eng, b - 3)
                c["on"].wait(eng, b - 2)
                eng.matmul(m_a[:, 0:P], wq_s[:, :], xcT[:, 0:D], start=True, stop=True)
                eng.matmul(m_b[:, 0:K], wk_s[:, :], xcT[:, D:D + K], start=True, stop=True)
                c["proj"].done(eng.matmul(m_b[0:K, P:2 * P], xcT[:, D:D + K], wv_s[:, :], start=True, stop=True))

            def scores(g):
                def run(b, q):
                    n, h = 4 * b + g, g % 2
                    r = slice(32 * g, 32 * g + 32)
                    if g == 0:
                        c["qT"].wait(eng, b + 1)
                        c["kz"].wait(eng, b + 1)
                    c["sub"].wait(eng, n - 1)
                    c["S"].done(eng.matmul(score_b[h][:, 0:4 * K], qT[r, q % 2, :],
                                           kz[r, q % 2, :, :].rearrange("p j k -> p (j k)"),
                                           start=True, stop=True, tile_position=(32 * g, 0)))
                return run

            def turn(g):
                def run(b, q):
                    n, h = 4 * b + g, g % 2
                    c["exp"].wait(eng, n + 1)
                    c["PT_e"].wait(eng, n - 1)
                    for j in range(4):
                        ins = eng.transpose(prT_b[h][0:K, j * P:j * P + P], prob[:, h, j, :], ident[:, :])
                    c["PT"].done(ins)
                return run

            def mix(g):
                def run(b, q):
                    n, h = 4 * b + g, g % 2
                    c["PT_e"].wait(eng, n + 1)
                    if g == 0:
                        c["v"].wait(eng, b + 1)
                        c["U"].wait(eng, b)
                    for j in range(4):
                        ins = eng.matmul(u_b[32 * j:32 * j + DH + 1, g * P:g * P + P],
                                         v1[0:K, q, 4 * g + j, :], pT[0:K, h, j, :],
                                         start=True, stop=True, tile_position=(0, 32 * j))
                    c["PV"].done(ins)
                return run

            def back(b, q):
                c["U"].wait(eng, b + 1)
                c["v"].wait(eng, upto_b(b + 3))
                for g in range(GROUPS):
                    ins = eng.transpose(m_b[:, g * P:g * P + P], uT[:, g, :], ident[:, :])
                c["OT"].done(ins)

            def heads(b, q):
                c["on"].wait(eng, b + 1)
                c["xn2T_e"].wait(eng, b)
                c["onT"].done(eng.transpose(m_c[:, 0:P], on[:, :], ident[:, :]))

            def out_proj(b, q):
                c["onT_e"].wait(eng, b + 1)
                c["O"].done(eng.matmul(m_c[:, 0:D], onT[:, :], wo_s[:, :], start=True, stop=True))

            def normed(b, q):
                c["xn2"].wait(eng, b + 1)
                c["carry"].wait(eng, b)
                c["row_of"].wait(eng, b)
                c["xn2T"].done(eng.transpose(m_c[:, 0:P], xn2[:, q % 2, :], ident[:, :]))

            def router(b, q):
                c["xn2T_e"].wait(eng, b + 1)
                c["ln1T_e"].wait(eng, upto_b(b + 5))
                c["logits"].done(eng.matmul(m_a[:, 0:E], xn2T[:, :], gate_s[:, :], start=True, stop=True))

            def ranks(b, q):
                c["sel"].wait(eng, b + 1)
                c["x2"].wait(eng, upto_b(b + 2))
                eng.matmul(m_c[:, 0:E], before[:, :], sel[:, :], start=True, stop=True)
                c["pos"].done(eng.matmul(m_c[:, E:2 * E], ones[:, :], sel[:, :], start=True, stop=True))

            batches(eng, [(g - 1, scores(g)) for g in range(4)] +
                    [(-4, project), (-6, inputs), (6, back), (7, heads), (8, out_proj), (10, normed),
                     (11, router), (13, ranks)] +
                    [(g + 1, turn(g)) for g in range(4)] + [(g + 2, mix(g)) for g in range(4)])

            table.wait(eng, 1)
            ffn_weights.wait(eng, N_FFN)

            def tokens(t, q):
                tile_in[q].landed(eng, t, q)
                f["xT_e"].wait(eng, t)
                f["xT"].done(eng.transpose(xT_b[:, 0:P], xs[:, q, 0:D], ident[:, :]))

            def up(t, q):
                h = q % 2
                f["xT_e"].wait(eng, t + 1)
                f["hid"].wait(eng, t - 1)
                settled(eng)
                e = eng.value_load(t_exp[0:1, bass.ds(t, 1)], min_val=0, max_val=E - 1)
                eng.matmul(h1_b[h][:, 0:HID], xsT[:, h, :], w1_s[:, bass.ds(e * HID, HID)], start=True, stop=True)
                f["h"].done(eng.matmul(h3_b[h][:, 0:HID], xsT[:, h, :], w3_s[:, bass.ds(e * HID, HID)],
                                       start=True, stop=True))

            def turn_hidden(t, q):
                h = q % 2
                f["hid"].wait(eng, t + 1)
                f["hT_e"].wait(eng, t - 1)
                for k in range(HC):
                    ins = eng.transpose(hT_b[h][0:CHUNK[k], k * P:k * P + P],
                                        hid[:, h, k * P:k * P + CHUNK[k]], ident[:, :])
                f["hT"].done(ins)

            def down(t, q):
                h = q % 2
                f["hT_e"].wait(eng, t + 1)
                f["y_e"].wait(eng, t)
                settled(eng)
                e = eng.value_load(t_exp[0:1, bass.ds(t, 1)], min_val=0, max_val=E - 1)
                for k in range(HC):
                    ins = eng.matmul(y_b[:, 0:D], hidT[0:CHUNK[k], h, k, :],
                                     w2_s[0:CHUNK[k], k, bass.ds(e * D, D)],
                                     start=(k == 0), stop=(k == HC - 1))
                f["y"].done(ins)

            tiles(eng, [(-1, tokens), (0, up), (1, turn_hidden), (2, down)])


def kernel(**inputs):
    import numpy as np
    import concourse.bacc as bacc
    from concourse.bass_utils import run_bass_kernel_spmd

    p = "L0_xattn_"
    laid = {
        "x": inputs["x"], "ctx_in": inputs["ctx_1024"],
        "wqT": inputs[p + "wq"].T, "bq": inputs[p + "bq"], "wkT": inputs[p + "wk"].T, "bk": inputs[p + "bk"],
        "wvT": inputs[p + "wv"].T, "bv": inputs[p + "bv"], "woT": inputs[p + "wo"].T, "bo": inputs[p + "bo"],
        "gateT": inputs["L0_ffn_gate_w"].T, "ebias": inputs["L0_ffn_expert_bias"],
        "w1": inputs["L0_ffn_w1"], "w2": inputs["L0_ffn_w2"], "w3": inputs["L0_ffn_w3"],
    }
    nc = bacc.Bacc("TRN2", target_bir_lowering=False, num_devices=1)
    arrays, args = {}, {}
    for name, value in laid.items():
        a = np.ascontiguousarray(value)
        arrays[f"in_{name}"] = a
        args[name] = nc.dram_tensor(f"in_{name}", a.shape, mybir.dt.from_np(a.dtype), kind="ExternalInput").ap()
    out = nc.dram_tensor("out_0", laid["x"].shape, F32, kind="ExternalOutput").ap()
    build(nc, out=out, **args)
    r = run_bass_kernel_spmd(nc, [arrays], core_ids=[0])
    return r.results[0]["out_0"]
```

```python
from contextlib import ExitStack

import concourse.bass as bass
from concourse import mybir

F32 = mybir.dt.float32
F32R = mybir.dt.float32r
BF16 = mybir.dt.bfloat16
I32 = mybir.dt.int32
U32 = mybir.dt.uint32
ALU = mybir.AluOpType
ACT = mybir.ActivationFunctionType
AX = mybir.AxisListType

P = 128
HEADS = 16
EPS = 1e-5


class Counter:

    def __init__(self, sem, step=1):
        self.sem, self.step = sem, step

    def done(self, ins):
        ins.then_inc(self.sem, self.step)

    def wait(self, eng, runs):
        if isinstance(runs, int) and runs <= 0:
            return
        eng.wait_ge(self.sem, runs * self.step)


class Ring(Counter):

    def __init__(self, sem, n, per=1):
        super().__init__(sem, 16)
        self.n, self.per = n, per

    def landed(self, eng, item, q):
        eng.wait_ge(self.sem, (item - q) * (16 * self.per // self.n) + 16 * self.per)

    def reusable(self, eng, item, q):
        if not (isinstance(item, int) and item < self.n):
            eng.wait_ge(self.sem, (item - q) * (16 * self.per // self.n))


def walk(eng, steps, per, unroll, first, last, low, high, total):

    def one(rnd, phase):
        for g in range(per):
            for slot, run in steps:
                if (slot - g) % per == 0:
                    back = (slot - g) // per
                    item = rnd - back
                    if isinstance(item, int) and not 0 <= item < total:
                        continue
                    run(item, (phase - back) % unroll)

    for r in range(first, low):
        one(r, r % unroll)
    with eng.Fori(0, (high - low) // unroll) as r:
        for u in range(unroll):
            one(r * unroll + (low + u), (low + u) % unroll)
    for r in range(high, last + 1):
        one(r, r % unroll)


def build(nc, x, ctx_in, wqT, bq, wkT, bk, wvT, bv, woT, bo, gateT, ebias, w1, w2, w3, out):
    B, S, D = x.shape
    K = ctx_in.shape[1]
    DH = D // HEADS
    E, _, HID = w1.shape
    T = B * S
    SCALE = float(DH) ** -0.5
    GROUPS = 4
    HC = (HID + P - 1) // P
    CHUNK = [min(P, HID - c * P) for c in range(HC)]
    CAP = T + P
    NT = 2 * T // P + E - 1
    SPARE = (E - 1) * P
    ROW = D + 1
    NOWHERE = 4 * T
    assert S == P and D == P and HEADS == 4 * GROUPS and DH == 8

    xs_dram = nc.dram_tensor("expert_rows", [E * CAP + SPARE, ROW], F32, kind="Internal").ap()
    y_dram = nc.dram_tensor("expert_results", [2 * T, D], F32, kind="Internal").ap()

    with ExitStack() as stack:
        def sb(name, shape, dt=F32):
            return stack.enter_context(nc.sbuf_tensor(name, shape, dt))

        def ps(name, shape, dt=F32):
            return stack.enter_context(nc.psum_tensor(name, shape, dt))

        names = iter(range(10 ** 6))

        def counter(name, step=1):
            return Counter(stack.enter_context(nc.semaphore(f"{name}_{next(names)}")), step)

        def ring(name, n, per=1):
            return Ring(stack.enter_context(nc.semaphore(name)), n, per)

        wq_s, wk_s, wv_s, wo_s = (sb(n, [P, D]) for n in ("wq_s", "wk_s", "wv_s", "wo_s"))
        gate_s = sb("gate_s", [P, E])
        bq_s, bk_s, bqs_s = sb("bq_s", [P, 1]), sb("bk_s", [P, 1]), sb("bqs_s", [P, 1])
        bv_s, bo_b, bo_sum, eb_b = sb("bv_s", [P, 1]), sb("bo_b", [P, D]), sb("bo_sum", [P, D]), sb("eb_b", [P, E])
        w1_s, w3_s = sb("w1_s", [P, E * HID]), sb("w3_s", [P, E * HID])
        w2_s = sb("w2_s", [P, HC, E * D])
        w1_h, w1_l = sb("w1_h", [P, E * HID], F32R), sb("w1_l", [P, E * HID], F32R)
        w3_h, w3_l = sb("w3_h", [P, E * HID], F32R), sb("w3_l", [P, E * HID], F32R)
        ident = sb("ident", [P, P])
        head1, headmask = sb("head1", [P, HEADS]), sb("headmask", [P, 4])
        before = sb("before", [P, P], BF16)
        ones = sb("ones", [P, P], BF16)
        iota_e = sb("iota_e", [P, E])
        minus_half = sb("minus_half", [P, 1])
        place_of = sb("place_of", [P, B, 2], I32)
        XB = 4
        x_s, c_s = sb("x_s", [P, XB, D]), sb("c_s", [P, XB, D])
        x2 = sb("x2", [P, B, D])
        st1, mv1, ve1 = sb("st1", [P, 6]), sb("mv1", [P, 2, 2]), sb("ve1", [P, 2])
        rs1, sh1 = sb("rs1", [P, 2]), sb("sh1", [P, 2])
        st2, mv2, ve2 = sb("st2", [P, 6]), sb("mv2", [P, 2, 2]), sb("ve2", [P, 2])
        rs2, sh2 = sb("rs2", [P, 2]), sb("sh2", [P, 2])
        xn = sb("xn", [P, 2, D])
        xcT = sb("xcT", [P, D + K])
        qT, kz = sb("qT", [P, 2, P]), sb("kz", [P, 2, 4, K])
        v1 = sb("v1", [P, 4, HEADS, DH + 1])
        nmx = sb("nmx", [P, 2, 4])
        prob = sb("prob", [P, GROUPS, 4, K])
        pT = sb("pT", [P, GROUPS, 4, P])
        uT = sb("uT", [P, GROUPS, P])
        rden, on, onT = sb("rden", [P, HEADS]), sb("on", [P, D]), sb("onT", [P, P])
        x2s = sb("x2s", [P, 2, D])
        xn2, xn2T = sb("xn2", [P, 4, D]), sb("xn2T", [P, P])
        lmax, ex, esum = sb("lmax", [P, 1]), sb("ex", [P, 2, E]), sb("esum", [P, 2])
        rsum, biased = sb("rsum", [P, 2]), sb("biased", [P, E])
        top, topi = sb("top", [P, 8]), sb("topi", [P, 8], U32)
        chosen = sb("chosen", [P, 2, 2, E], BF16)
        gate_w, gates = sb("gate_w", [P, 2, E]), sb("gates", [P, 2, 2])
        pos = sb("pos", [P, 2, E])
        row_of = sb("row_of", [P, 2, 2, E])
        place_w, places = sb("place_w", [P, 2, E]), sb("places", [P, 2, 2], I32)
        rows = sb("rows", [P, 2, 2, ROW])
        region_less = sb("region_less", [1, E])
        upto_e = sb("upto_e", [1, E, E])
        cnt, ntile, jump = sb("cnt", [1, E], I32), sb("ntile", [1, E], I32), sb("jump", [1, E])
        part, upto = sb("part", [1, E, E]), sb("upto", [1, E])
        tvec, passed, skip = sb("tvec", [1, NT]), sb("passed", [1, NT]), sb("skip", [1, NT])
        passes = w1_s[0:1, 0:NT * E].rearrange("p (t e) -> p t e", e=E)
        skips = w1_s[0:1, NT * E:2 * NT * E].rearrange("p (t e) -> p t e", e=E)
        ends = sb("ends", [1, E], I32)
        t_exp, t_row = sb("t_exp", [1, 4 + (NT + 3) // 4 * 4], I32), sb("t_row", [1, NT], I32)
        padding = sb("padding", [P, ROW])
        xs = sb("xs", [P, 4, ROW])
        where = sb("where", [P, 4], I32)
        xsT_h, xsT_l = sb("xsT_h", [P, 4, P], F32R), sb("xsT_l", [P, 4, P], F32R)
        act, hid = sb("act", [P, 2, HID]), sb("hid", [P, 2, HID])
        hidT = sb("hidT", [P, 2, HC, P])
        y_s = sb("y_s", [P, 4, D])
        LG = 4
        both = w1_s[:, 0:2 * LG * 2 * D].rearrange("p (n t k d) -> p n t k d", n=2, t=LG, k=2)
        tot = w3_s[:, 0:2 * LG * D].rearrange("p (n t d) -> p n t d", n=2, t=LG)

        bank = [ps(f"bank{n}", [P, 512]) for n in range(8)]
        score_b, prT_b, u_b, m_a, m_b, m_c = bank[0:2], bank[2:4], bank[4], bank[5], bank[6], bank[7]
        h1_b, h3_b, hT_b, y_b, xT_b = bank[0:2], bank[2:4], bank[4:6], bank[6], bank[7]

        weights, ffn_weights, consts = counter("weights", 16), counter("ffn_weights", 16), counter("consts")
        mask_r, ready, bo_p, bo_ready = (counter(n) for n in ("mask_r", "ready", "bo_p", "bo_ready"))
        spare_r = counter("spare_r", 16)
        weights_h, weights_l = counter("weights_h"), counter("weights_l")
        c = {n: counter(n) for n in (
            "stats1 var1 eps1 rstd1 shift1 xn xbo ln1T ln1T_e proj qT kz v S max sub exp PT PT_e PV U OT rden on "
            "onT onT_e O x2 keep stats2 var2 eps2 rstd2 shift2 xn2 xn2T xn2T_e logits lmax ex rsum biased top "
            "topi chosen gate_w gates pos pos_e row_of place_w places rows1 rows2 placed").split()}
        loads = [ring(f"loads{n}", XB, 2) for n in range(XB)]
        scat = [ring(f"scat{n}", 2, 2) for n in range(2)]
        table, ended, padded, pad_rows = counter("table"), counter("ended"), counter("padded", 16), counter("pad_rows")
        f = {n: counter("f_" + n) for n in "xT xT_h xT_l where h act hid hT hT_e y y_e".split()}
        tile_in = [ring(f"tile_in{n}", 4) for n in range(4)]
        tile_out = [ring(f"tile_out{n}", 4) for n in range(4)]
        y_in = [ring(f"y_in{n}", 2) for n in range(2)]
        added, total, stored = counter("added"), counter("total"), [ring(f"stored{n}", 2) for n in range(2)]
        block = stack.enter_context(nc.Block())

        N_WEIGHTS, N_FFN, N_CONSTS = 10, 2 + HC, 18

        def batches(eng, steps):
            walk(eng, steps, GROUPS, 4, -4, B + 5, 8, B - 4, B)

        def tiles(eng, steps):
            walk(eng, steps, 1, 4, -2, NT + 1, 6, 6 + (NT - 8) // 4 * 4, NT)

        PARTS = [tuple(w[:, n * HID * E // 2:(n + 1) * HID * E // 2] for w in ws)
                 for ws in ((w1_s, w1_h, w1_l), (w3_s, w3_h, w3_l)) for n in range(2)]
        SPLIT_AT = [2, 3, 4, 5]

        def three_passes(eng, out, lhs, rhs):
            (lh, ll), (rh, rl) = lhs, rhs
            eng.matmul(out, lh, rh, start=True, stop=False)
            eng.matmul(out, lh, rl, start=False, stop=False)
            return eng.matmul(out, ll, rh, start=False, stop=True)

        BY_HEAD = (3,)

        def sub_runs(b, g):
            return (4 - len(BY_HEAD)) * b + sum(j not in BY_HEAD for j in range(g + 1))

        def scores_out(eng, b, g):
            if (g - 2) % 4 in BY_HEAD:
                c["exp"].wait(eng, 4 * b + g - 1)
            else:
                c["sub"].wait(eng, sub_runs(b - (g < 2), (g - 2) % 4))

        def settled(eng):
            eng.nop(nofuse=True)

        def upto_b(n):
            return min(n, B) if isinstance(n, int) else n

        @block.sync
        def _(eng):
            for dst, src in ((wq_s, wqT), (wk_s, wkT), (wv_s, wvT), (wo_s, woT), (gate_s, gateT)):
                weights.done(eng.dma_start(dst[:, :], src))
            for dst, src in ((bq_s, bq), (bk_s, bk), (bv_s, bv)):
                weights.done(eng.dma_start(dst[:, :], src.rearrange("(p a) -> p a", a=1)))
            for dst, src in ((bo_b, bo), (eb_b, ebias)):
                n = src.shape[0]
                weights.done(eng.dma_start(dst[:, :], src.rearrange("(a n) -> a n", a=1).broadcast_to((P, n))))

            def load(b, q):
                for step in ("xn", "xbo", "ln1T"):
                    c[step].wait(eng, b - XB + 1)
                loads[q].done(eng.dma_start(x_s[:, q, :], x[bass.ds(b, 1), :, :].rearrange("a s d -> (a s) d")))
                loads[q].done(eng.dma_start(c_s[0:K, q, :],
                                            ctx_in[bass.ds(b, 1), :, :].rearrange("a s d -> (a s) d")))

            for b in range(XB):
                load(b, b)
            for dst, src in ((w1_s, w1), (w3_s, w3)):
                ffn_weights.done(eng.dma_start(dst[:, :].rearrange("p (e h) -> p e h", e=E),
                                               src.rearrange("e p h -> p e h")))
            for h in range(HC):
                ffn_weights.done(eng.dma_start(
                    w2_s[0:CHUNK[h], h, :].rearrange("p (e n) -> p e n", e=E),
                    w2[:, h * P:h * P + CHUNK[h], :].rearrange("e p n -> p e n")))
            pad_rows.wait(eng, 2)
            for n in range(E - 1):
                r = E * CAP + n * P
                spare_r.done(eng.dma_start(xs_dram[r:r + P, :], padding[:, :]))
            with eng.Fori(1, B // XB) as r:
                for q in range(XB):
                    load(r * XB + q, q)

            ended.wait(eng, 1)
            end_rows = [eng.alloc_register(f"end_row{e}") for e in range(E)]
            eng.load(end_rows, ends[0:1, :])
            for reg in end_rows:
                row = bass.RuntimeValue.of_register_unchecked(reg).with_bounds(min_val=0, max_val=E * CAP - P)
                padded.done(eng.dma_start(xs_dram[bass.ds(row, P), :], padding[:, :]))

            for n in range(2):
                scat[n].wait(eng, B)
            padded.wait(eng, E)
            spare_r.wait(eng, E - 1)
            table.wait(eng, 1)

            def tile_load(t, q):
                f["xT"].wait(eng, t - 3)
                f["where"].wait(eng, t - 3)
                row = eng.value_load(t_row[0:1, bass.ds(t, 1)], min_val=0, max_val=E * CAP + SPARE - P)
                tile_in[q].done(eng.dma_start(xs[:, q, :], xs_dram[bass.ds(row, P), :]))

            for t in range(4):
                tile_load(t, t)
            last = NT // 4 * 4
            with eng.Fori(1, last // 4) as r:
                for q in range(4):
                    tile_load(r * 4 + q, q)
            for t in range(last, NT):
                tile_load(t, t % 4)

            for q in range(4):
                tile_out[q].wait(eng, (NT - q + 3) // 4)

            def y_load(n, q):
                added.wait(eng, n - 1)
                src = y_dram.rearrange("(p b k) d -> p b k d", p=P, k=2)[:, bass.ds(n * LG, LG), :, :]
                y_in[q].done(eng.dma_start(both[:, q, :, :, :], src))

            for n in range(2):
                y_load(n, n)
            with eng.Fori(1, B // LG // 2) as r:
                for q in range(2):
                    y_load(r * 2 + q, q)

        @block.gpsimd
        def _(eng):
            pad_rows.done(eng.memset(padding[:, 0:D], 0.0))
            pad_rows.done(eng.memset(padding[:, D:ROW].bitcast(I32), NOWHERE))
            made = [0]

            def const(ins):
                consts.done(ins)
                made[0] += 1
                consts.wait(eng, made[0])

            const(eng.memset(minus_half[:, :], -0.5))
            const(eng.memset(ident[:, :], 0.0))
            const(eng.affine_select(out=ident[:, :], in_=ident[:, :], compare_op=ALU.not_equal, fill=1.0,
                                    base=0, pattern=[[-1, P]], channel_multiplier=1))
            const(eng.memset(head1[:, :], 1.0))
            const(eng.affine_select(out=head1[:, :], in_=head1[:, :], compare_op=ALU.is_ge, fill=0.0,
                                    base=0, pattern=[[-DH, HEADS]], channel_multiplier=1))
            const(eng.affine_select(out=head1[:, :], in_=head1[:, :], compare_op=ALU.is_ge, fill=0.0,
                                    base=DH - 1, pattern=[[DH, HEADS]], channel_multiplier=-1))
            const(eng.memset(before[:, :], 1.0))
            const(eng.affine_select(out=before[:, :], in_=before[:, :], compare_op=ALU.is_gt, fill=0.0,
                                    base=0, pattern=[[1, P]], channel_multiplier=-1))
            const(eng.memset(ones[:, :], 1.0))
            const(eng.iota(iota_e[:, :], [[1, E]], base=0, channel_multiplier=0,
                           allow_small_or_imprecise_dtypes=True))
            const(eng.iota(region_less[:, :], [[CAP, E]], base=1 - P, channel_multiplier=0,
                           allow_small_or_imprecise_dtypes=True))
            const(eng.memset(upto_e[:, :, :], 1.0))
            const(eng.affine_select(out=upto_e[:, :, :], in_=upto_e[:, :, :], compare_op=ALU.is_ge, fill=0.0,
                                    base=0, pattern=[[1, E], [-1, E]], channel_multiplier=0))
            const(eng.iota(row_of[:, 1, 1, :], [[CAP, E]], base=0, channel_multiplier=0,
                           allow_small_or_imprecise_dtypes=True))
            const(eng.iota(place_of[:, :, :], [[2, B], [1, 2]], base=0, channel_multiplier=2 * B))
            const(eng.iota(tvec[:, :], [[1, NT]], base=0, channel_multiplier=0,
                           allow_small_or_imprecise_dtypes=True))
            const(eng.memset(v1[:, :, :, :], 1.0))
            const(eng.memset(xcT[:, :], 0.0))
            assert made[0] == N_CONSTS
            weights.wait(eng, N_WEIGHTS)

            def rstd(n, mv, ve, rs, sh):
                def run(b, q):
                    h = q % 2
                    c[f"var{n}"].wait(eng, b + 1)
                    c["xn" if n == 1 else "xn2"].wait(eng, b - 1)
                    settled(eng)
                    c[f"eps{n}"].done(eng.tensor_scalar(ve[:, h:h + 1], mv[:, h, 1:2], EPS, None, ALU.add))
                    c[f"eps{n}"].wait(eng, b + 1)
                    c[f"rstd{n}"].done(eng.tensor_tensor(rs[:, h:h + 1], ve[:, h:h + 1], minus_half[:, :],
                                                         ALU.pow))
                    c[f"rstd{n}"].wait(eng, b + 1)
                    settled(eng)
                    c[f"shift{n}"].done(eng.tensor_scalar(sh[:, h:h + 1], mv[:, h, 0:1], rs[:, h:h + 1], -1.0,
                                                          ALU.mult, ALU.mult))
                return run

            def keep_input(b, q):
                loads[q].landed(eng, b, q)
                c["xbo"].done(eng.tensor_tensor(x2[:, bass.ds(b, 1), :].rearrange("p a d -> p (a d)"),
                                                x_s[:, q, :], bo_sum[:, :], ALU.add))

            def keep(b, q):
                c["x2"].wait(eng, b + 1)
                settled(eng)
                c["keep"].done(eng.tensor_copy(x2[:, bass.ds(b, 1), :].rearrange("p a d -> p (a d)"),
                                               x2s[:, q % 2, :]))

            def scatter(b, q):
                h = q % 2
                scat[h].reusable(eng, b, h)
                c["gates"].wait(eng, b + 1)
                c["xn2"].wait(eng, b + 1)
                settled(eng)
                for k in range(2):
                    c[f"rows{k + 1}"].done(eng.tensor_scalar(rows[:, h, k, 0:D], xn2[:, q, :],
                                                             gates[:, h, k:k + 1], rsum[:, h:h + 1],
                                                             ALU.mult, ALU.mult))
                c["placed"].done(eng.tensor_copy(
                    rows[:, h, :, D:ROW].bitcast(I32),
                    place_of[:, bass.ds(b, 1), :].rearrange("p a k -> p k a")))
                c["rows2"].wait(eng, b + 1)
                c["placed"].wait(eng, b + 1)
                c["places"].wait(eng, b + 1)
                settled(eng)
                for k in range(2):
                    scat[h].done(eng.indirect_dma_start(
                        xs_dram, bass.IndirectOffsetOnAxis(ap=places[:, h, k:k + 1], axis=0),
                        rows[:, h, k, :], None))

            bo_ready.wait(eng, 1)
            batches(eng, [(-10, rstd(1, mv1, ve1, rs1, sh1)), (12, rstd(2, mv2, ve2, rs2, sh2)), (13, keep),
                          (-11, keep_input), (27, scatter)])

            def keep_places(t, q):
                tile_in[q].landed(eng, t, q)
                tile_out[q].reusable(eng, t, q)
                settled(eng)
                f["where"].done(eng.tensor_copy(where[:, q:q + 1], xs[:, q, D:ROW].bitcast(I32)))

            def results(t, q):
                f["y_e"].wait(eng, t + 1)
                f["where"].wait(eng, t + 1)
                settled(eng)
                tile_out[q].done(eng.indirect_dma_start(
                    y_dram, bass.IndirectOffsetOnAxis(ap=where[:, q:q + 1], axis=0), y_s[:, q, :], None,
                    bounds_check=2 * T - 1, oob_is_err=False))

            tiles(eng, [(2, results), (-1, keep_places)])

        @block.vector
        def _(eng):
            consts.wait(eng, N_CONSTS)
            weights.wait(eng, N_WEIGHTS)
            mask_r.done(eng.tensor_reduce(headmask[:, :], head1[:, :].rearrange("p (g j) -> p j g", j=4),
                                          AX.X, ALU.add))
            mask_r.wait(eng, 1)
            ready.done(eng.tensor_scalar(bqs_s[:, :], bq_s[:, :], SCALE, None, ALU.mult))
            ready.done(eng.memset(u_b[:, :], 0.0))

            bo_p.wait(eng, 1)
            bo_ready.done(eng.tensor_tensor(bo_sum[:, :], bo_b[:, :], m_c[:, 0:D], ALU.add))

            def stats1(b, q):
                loads[q].landed(eng, b, q)
                c["var1"].wait(eng, b)
                settled(eng)
                c["stats1"].done(eng.bn_stats(st1[:, :], x_s[:, q, :]))

            def var1(b, q):
                c["stats1"].wait(eng, b + 1)
                c["xn"].wait(eng, b - 1)
                settled(eng)
                c["var1"].done(eng.bn_aggr(mv1[:, q % 2, :], st1[:, :]))

            def keys(b, q):
                h = q % 2
                c["proj"].wait(eng, b + 1)
                c["S"].wait(eng, 4 * b - 4)
                c["kz"].done(eng.scalar_tensor_tensor(
                    out=kz[:, h, :, :], in0=m_b[:, 0:K].unsqueeze(1).broadcast_to((P, 4, K)),
                    scalar=bk_s[:, 0:1], in1=headmask[:, :].unsqueeze(2).broadcast_to((P, 4, K)),
                    op0=ALU.add, op1=ALU.mult))

            def maxima(g):
                def run(b, q):
                    n, h = 4 * b + g, g % 2
                    c["S"].wait(eng, n + 1)
                    scores_out(eng, b, g)
                    c["max"].done(eng.tensor_reduce(nmx[:, h, :], score_b[h][:, 0:4 * K].rearrange(
                        "p (j k) -> p j k", j=4), AX.X, ALU.max, negate=True))
                return run

            def shifted(g):
                def run(b, q):
                    n, h = 4 * b + g, g % 2
                    c["max"].wait(eng, n + 1)
                    c["PT"].wait(eng, n - 3)
                    c["sub"].done(eng.tensor_tensor(
                        prob[:, g, :, :], score_b[h][:, 0:4 * K].rearrange("p (j k) -> p j k", j=4),
                        nmx[:, h, :].unsqueeze(2).broadcast_to((P, 4, K)), ALU.add))
                return run

            def denominators(b, q):
                c["OT"].wait(eng, b + 1)
                c["on"].wait(eng, b)
                c["rden"].done(eng.reciprocal(rden[:, :].unsqueeze(2), o_all[:, :, DH:DH + 1]))

            def divide(b, q):
                c["rden"].wait(eng, b + 1)
                c["onT"].wait(eng, b)
                c["on"].done(eng.tensor_tensor(on[:, :].rearrange("p (n d) -> p n d", d=DH), o_all[:, :, 0:DH],
                                               rden[:, :].unsqueeze(2).broadcast_to((P, HEADS, DH)), ALU.mult))

            def residual(b, q):
                c["O"].wait(eng, b + 1)
                c["xbo"].wait(eng, b + 1)
                c["keep"].wait(eng, b - 1)
                c["xn2"].wait(eng, b - 1)
                c["x2"].done(eng.tensor_tensor(x2s[:, q % 2, :], m_c[:, 0:D],
                                               x2[:, bass.ds(b, 1), :].rearrange("p a d -> p (a d)"), ALU.add))

            def stats2(b, q):
                c["x2"].wait(eng, b + 1)
                c["var2"].wait(eng, b)
                settled(eng)
                c["stats2"].done(eng.bn_stats(st2[:, :], x2s[:, q % 2, :]))

            def var2(b, q):
                c["stats2"].wait(eng, b + 1)
                c["xn2"].wait(eng, b - 1)
                settled(eng)
                c["var2"].done(eng.bn_aggr(mv2[:, q % 2, :], st2[:, :]))

            def logit_max(b, q):
                c["logits"].wait(eng, b + 1)
                c["ex"].wait(eng, b)
                c["lmax"].done(eng.tensor_reduce(lmax[:, :], m_a[:, 0:E], AX.X, ALU.max, negate=True))

            def share(b, q):
                h = q % 2
                c["ex"].wait(eng, b + 1)
                c["rows2"].wait(eng, b - 1)
                c["rsum"].done(eng.reciprocal(rsum[:, h:h + 1], esum[:, h:h + 1]))

            def bias(b, q):
                h = q % 2
                c["rsum"].wait(eng, b + 1)
                c["topi"].wait(eng, b)
                c["biased"].done(eng.scalar_tensor_tensor(out=biased[:, :], in0=ex[:, h, :],
                                                          scalar=rsum[:, h:h + 1], in1=eb_b[:, :],
                                                          op0=ALU.mult, op1=ALU.add))

            def best(b, q):
                c["biased"].wait(eng, b + 1)
                c["topi"].wait(eng, b)
                settled(eng)
                c["top"].done(eng.max(top[:, :], biased[:, :]))

            def best_index(b, q):
                c["top"].wait(eng, b + 1)
                c["chosen"].wait(eng, b)
                settled(eng)
                c["topi"].done(eng.max_index(topi[:, :], top[:, :], biased[:, :]))

            def one_hot(b, q):
                c["topi"].wait(eng, b + 1)
                c["pos"].wait(eng, b - 1)
                c["place_w"].wait(eng, b - 1)
                c["chosen"].done(eng.tensor_tensor(
                    chosen[:, q % 2, :, :], iota_e[:, :].unsqueeze(1).broadcast_to((P, 2, E)),
                    topi[:, 0:2].unsqueeze(2).broadcast_to((P, 2, E)), ALU.is_equal))

            def gate_parts(b, q):
                h = q % 2
                c["chosen"].wait(eng, b + 1)
                c["gates"].wait(eng, b)
                c["gate_w"].done(eng.tensor_tensor(gate_w[:, :, :], chosen[:, h, :, :],
                                                   ex[:, h, :].unsqueeze(1).broadcast_to((P, 2, E)), ALU.mult))

            def gate_sums(b, q):
                c["gate_w"].wait(eng, b + 1)
                c["rows2"].wait(eng, b - 1)
                c["gates"].done(eng.tensor_reduce(gates[:, q % 2, :], gate_w[:, :, :], AX.X, ALU.add))

            def rank(b, q):
                h = q % 2
                c["pos_e"].wait(eng, b + 1)
                c["row_of"].wait(eng, b)
                c["place_w"].wait(eng, b - 1)
                c["row_of"].done(eng.tensor_tensor(
                    row_of[:, h, :, :], pos[:, :, :],
                    row_of[:, 1 - h, 1, :].unsqueeze(1).broadcast_to((P, 2, E)), ALU.add))

            def place_parts(b, q):
                h = q % 2
                c["row_of"].wait(eng, b + 1)
                c["places"].wait(eng, b)
                c["place_w"].done(eng.tensor_tensor(
                    place_w[:, :, :], chosen[:, h, :, :],
                    row_of[:, h, 0, :].unsqueeze(1).broadcast_to((P, 2, E)), ALU.mult))

            def place_sums(b, q):
                h = q % 2
                c["place_w"].wait(eng, b + 1)
                scat[h].reusable(eng, b, h)
                with nc.allow_low_precision(reason="row numbers are whole and below 2**24"):
                    c["places"].done(eng.tensor_reduce(places[:, h, :], place_w[:, :, :], AX.X, ALU.add))

            def low_parts(b, q):
                if isinstance(b, int) and b in SPLIT_AT:
                    n = SPLIT_AT.index(b)
                    whole, high, low = PARTS[n]
                    weights_h.wait(eng, n + 1)
                    weights_l.done(eng.tensor_tensor(low, whole, high, ALU.subtract))

            o_all = m_b[:, :].rearrange("p (n w) -> p n w", w=32)
            batches(eng, [(g, maxima(g)) for g in range(4)] +
                    [(-13, stats1), (11, residual), (12, var2), (20, logit_max), (22, bias), (23, best_index),
                     (24, gate_parts), (26, rank), (27, place_sums), (8, denominators)] +
                    [(g, shifted(g)) for g in range(4) if g not in BY_HEAD] +
                    [(-11, var1), (-2, keys), (8, divide), (11, stats2), (21, share), (22, best),
                     (23, one_hot), (24, gate_sums), (26, place_parts), (3, low_parts)])

            made = [0]

            def link(ins):
                c["row_of"].done(ins)
                made[0] += 1
                c["row_of"].wait(eng, B + made[0])

            def sums(out, parts):
                link(eng.tensor_reduce(out, parts, AX.X, ALU.add))

            c["row_of"].wait(eng, B)
            c["keep"].wait(eng, B)
            final = row_of[0:1, (B - 1) % 2, 1, :]
            ended.done(eng.tensor_copy(ends[:, :], final))
            link(eng.memset(t_exp[:, :], 0))
            link(eng.tensor_tensor(cnt[:, :], final, region_less[:, :], ALU.subtract))
            link(eng.tensor_scalar(ntile[:, :], cnt[:, :], P.bit_length() - 1, None, ALU.logical_shift_right))
            link(eng.tensor_scalar(jump[:, :], ntile[:, :], -float(P), float(CAP), ALU.mult, ALU.add))
            link(eng.tensor_tensor(part[:, :, :], upto_e[:, :, :],
                                   ntile[:, :].unsqueeze(1).broadcast_to((1, E, E)), ALU.mult))
            sums(upto[:, :], part[:, :, :])
            link(eng.tensor_tensor(passes, tvec[:, :].unsqueeze(2).broadcast_to((1, NT, E)),
                                   upto[:, :].unsqueeze(1).broadcast_to((1, NT, E)), ALU.is_ge))
            sums(passed[:, :], passes)
            link(eng.tensor_scalar(t_exp[:, 4:4 + NT], passed[:, :], float(E - 1), None, ALU.min))
            link(eng.tensor_tensor(skips, passes, jump[:, :].unsqueeze(1).broadcast_to((1, NT, E)), ALU.mult))
            sums(skip[:, :], skips)
            table.done(eng.scalar_tensor_tensor(out=t_row[:, :], in0=tvec[:, :], scalar=float(P),
                                                in1=skip[:, :], op0=ALU.mult, op1=ALU.add))
            for b in hT_b:
                table.done(eng.memset(b[:, :], 0.0))

            def gated(t, q):
                h = q % 2
                f["act"].wait(eng, t + 1)
                f["hT"].wait(eng, t - 1)
                f["hid"].done(eng.tensor_tensor(hid[:, h, :], h3_b[h][:, 0:HID], act[:, h, :], ALU.mult))

            def hidden(t, q):
                h = q % 2
                f["hT"].wait(eng, t + 1)
                f["y"].wait(eng, t - 1)
                f["hT_e"].done(eng.tensor_copy(hidT[:, h, :, :],
                                               hT_b[h][:, 0:HC * P].rearrange("p (c t) -> p c t", c=HC)))

            def tokens_low(t, q):
                f["xT_h"].wait(eng, t + 1)
                f["h"].wait(eng, t - 3)
                f["xT_l"].done(eng.tensor_tensor(xsT_l[:, q, :], xT_b[:, 0:P], xsT_h[:, q, :], ALU.subtract))

            tiles(eng, [(1, hidden), (-2, tokens_low), (0, gated)])

            def add_up(n, q):
                y_in[q].landed(eng, n, q)
                stored[q].reusable(eng, n, q)
                added.done(eng.tensor_tensor(tot[:, q, :, :], both[:, q, :, 0, :], both[:, q, :, 1, :], ALU.add))
                added.wait(eng, n + 1)
                total.done(eng.tensor_tensor(tot[:, q, :, :], tot[:, q, :, :],
                                             x2[:, bass.ds(n * LG, LG), :], ALU.add))

            for n in range(2):
                add_up(n, n)
            with eng.Fori(1, B // LG // 2) as r:
                for q in range(2):
                    add_up(r * 2 + q, q)

        @block.scalar
        def _(eng):
            ready.wait(eng, 2)

            def exps(g):
                def run(b, q):
                    n, h = 4 * b + g, g % 2
                    if g in BY_HEAD:
                        c["max"].wait(eng, n + 1)
                        c["PT"].wait(eng, n - 3)
                        for j in range(4):
                            ins = eng.activation(prob[:, g, j, :], score_b[h][:, j * K:j * K + K], ACT.Exp,
                                                 bias=nmx[:, h, j:j + 1])
                        c["exp"].done(ins)
                    else:
                        c["sub"].wait(eng, sub_runs(b, g))
                        c["exp"].done(eng.activation(prob[:, g, :, :], prob[:, g, :, :], ACT.Exp))
                return run

            def probs(g):
                def run(b, q):
                    n, h = 4 * b + g, g % 2
                    c["PT"].wait(eng, n + 1)
                    c["PV"].wait(eng, n - 3)
                    c["PT_e"].done(eng.activation(pT[0:K, g, :, :],
                                                  prT_b[h][0:K, :].rearrange("k (j t) -> k j t", j=4), ACT.Copy))
                return run

            def inputs(b, q):
                c["ln1T"].wait(eng, b + 1)
                c["proj"].wait(eng, b)
                c["ln1T_e"].done(eng.activation(xcT[:, :], m_a[:, 0:D + K], ACT.Copy))

            def queries(b, q):
                h = q % 2
                c["proj"].wait(eng, b + 1)
                c["S"].wait(eng, 4 * b - 4)
                c["qT"].done(eng.activation(qT[:, h, :], m_a[:, 0:P], ACT.Identity, bias=bqs_s[:, 0:1],
                                            scale=SCALE))

            def values(b, q):
                c["kz"].wait(eng, b + 1)
                c["PV"].wait(eng, 4 * b - 12)
                c["v"].done(eng.activation(v1[0:K, q, :, 0:DH],
                                           m_b[0:K, P:2 * P].rearrange("p (n d) -> p n d", d=DH), ACT.Copy))

            def normalise(n, src, mv_done, dst_ring, dst):
                def run(b, q):
                    h = q % 2
                    c[f"shift{n}"].wait(eng, b + 1)
                    if n == 1:
                        c["ln1T"].wait(eng, b - 1)
                    else:
                        c["rows2"].wait(eng, b - 3)
                    c[mv_done].done(eng.activation(dst[:, q % dst_ring, :], src(q), ACT.Identity,
                                                   bias=(sh1, sh2)[n - 1][:, h:h + 1],
                                                   scale=(rs1, rs2)[n - 1][:, h:h + 1]))
                return run

            def high_parts(b, q):
                if isinstance(b, int) and b in SPLIT_AT:
                    whole, high, low = PARTS[SPLIT_AT.index(b)]
                    ffn_weights.wait(eng, N_FFN)
                    weights_h.done(eng.activation(high, whole, ACT.Copy))

            def context(b, q):
                c["PV"].wait(eng, 4 * b + 4)
                c["OT"].wait(eng, b)
                c["U"].done(eng.activation(uT[:, :, :], u_b[:, :].rearrange("p (g t) -> p g t", g=GROUPS),
                                           ACT.Copy))

            def heads(b, q):
                c["onT"].wait(eng, b + 1)
                c["O"].wait(eng, b)
                c["onT_e"].done(eng.activation(onT[:, :], m_c[:, 0:P], ACT.Copy))

            def normed(b, q):
                c["xn2T"].wait(eng, b + 1)
                c["logits"].wait(eng, b)
                c["xn2T_e"].done(eng.activation(xn2T[:, :], m_c[:, 0:P], ACT.Copy))

            def ranks(b, q):
                c["pos"].wait(eng, b + 1)
                c["xn2T"].wait(eng, upto_b(b + 3))
                c["row_of"].wait(eng, b)
                c["pos_e"].done(eng.activation(pos[:, :, :],
                                               m_c[:, P:P + 2 * E].rearrange("p (a e) -> p a e", a=2), ACT.Copy))

            def router(b, q):
                h = q % 2
                c["lmax"].wait(eng, b + 1)
                c["gate_w"].wait(eng, b - 1)
                c["ex"].done(eng.activation(ex[:, h, :], m_a[:, 0:E], ACT.Exp, bias=lmax[:, 0:1],
                                            accum_out=esum[:, h:h + 1]))

            batches(eng, [(g, exps(g)) for g in range(4)] +
                    [(20, router), (-8, normalise(1, lambda q: x_s[:, q, :], "xn", 2, xn)),
                     (15, normalise(2, lambda q: x2s[:, q % 2, :], "xn2", 4, xn2)),
                     (-3, queries), (9, heads), (-6, inputs), (-2, values), (16, normed), (24, ranks)] +
                    [(g + 1, probs(g)) for g in range(4)] + [(5, context), (2, high_parts)])

            def tokens_high(t, q):
                f["xT"].wait(eng, t + 1)
                f["h"].wait(eng, t - 3)
                f["xT_h"].done(eng.activation(xsT_h[:, q, :], xT_b[:, 0:P], ACT.Copy))

            def silu(t, q):
                h = q % 2
                f["h"].wait(eng, t + 1)
                f["hid"].wait(eng, t - 1)
                f["act"].done(eng.activation(act[:, h, :], h1_b[h][:, 0:HID], ACT.Silu))

            def result(t, q):
                f["y"].wait(eng, t + 1)
                tile_out[q].reusable(eng, t, q)
                f["y_e"].done(eng.activation(y_s[:, q, :], y_b[:, 0:D], ACT.Copy))

            tiles(eng, [(0, silu), (-2, tokens_high), (2, result)])

            def store(n, q):
                total.wait(eng, n + 1)
                dst = out.rearrange("b s d -> s b d")[:, bass.ds(n * LG, LG), :]
                stored[q].done(eng.dma_start(dst, tot[:, q, :, :]))

            with eng.Fori(0, B // LG // 2) as r:
                for q in range(2):
                    store(r * 2 + q, q)
            for q in range(2):
                stored[q].wait(eng, B // LG // 2)

        @block.tensor
        def _(eng):
            ready.wait(eng, 2)
            bo_p.done(eng.matmul(m_c[:, 0:D], bv_s[:, 0:1].broadcast_to((P, P)), wo_s[:, :],
                                 start=True, stop=True))
            bo_ready.wait(eng, 1)

            def keep_clock_up(n):
                for _ in range(n):
                    eng.matmul(m_c[:, :], ones[:, :], ones[:, 0:1].broadcast_to((P, 512)), start=True, stop=True)

            def inputs(b, q):
                h = q % 2
                c["xn"].wait(eng, b + 1)
                c["qT"].wait(eng, b)
                eng.transpose(m_a[:, 0:D], xn[:, h, :], ident[:, :])
                c["ln1T"].done(eng.transpose(m_a[:, D:D + K], c_s[0:K, q, :], ident[0:K, 0:K]))

            def project(b, q):
                c["ln1T_e"].wait(eng, b + 1)
                c["ex"].wait(eng, b - 5)
                c["v"].wait(eng, b)
                c["on"].wait(eng, b - 2)
                eng.matmul(m_a[:, 0:P], wq_s[:, :], xcT[:, 0:D], start=True, stop=True)
                eng.matmul(m_b[:, 0:K], wk_s[:, :], xcT[:, D:D + K], start=True, stop=True)
                c["proj"].done(eng.matmul(m_b[0:K, P:2 * P], xcT[:, D:D + K], wv_s[:, :], start=True, stop=True))

            def scores(g):
                def run(b, q):
                    n, h = 4 * b + g, g % 2
                    r = slice(32 * g, 32 * g + 32)
                    if g == 0:
                        if isinstance(b, int) and b == 0:
                            keep_clock_up(16)
                        c["qT"].wait(eng, b + 1)
                        c["kz"].wait(eng, b + 1)
                    scores_out(eng, b, g)
                    c["S"].done(eng.matmul(score_b[h][:, 0:4 * K], qT[r, q % 2, :],
                                           kz[r, q % 2, :, :].rearrange("p j k -> p (j k)"),
                                           start=True, stop=True, tile_position=(32 * g, 0)))
                return run

            def turn(g):
                def run(b, q):
                    n, h = 4 * b + g, g % 2
                    c["exp"].wait(eng, n + 1)
                    c["PT_e"].wait(eng, n - 1)
                    for j in range(4):
                        ins = eng.transpose(prT_b[h][0:K, j * P:j * P + P], prob[:, g, j, :], ident[:, :])
                    c["PT"].done(ins)
                return run

            def mix(g):
                def run(b, q):
                    n, h = 4 * b + g, g % 2
                    c["PT_e"].wait(eng, n + 1)
                    if g == 0:
                        c["v"].wait(eng, b + 1)
                        c["U"].wait(eng, b)
                    for j in range(4):
                        ins = eng.matmul(u_b[32 * j:32 * j + DH + 1, g * P:g * P + P],
                                         v1[0:K, q, 4 * g + j, :], pT[0:K, g, j, :],
                                         start=True, stop=True, tile_position=(0, 32 * j))
                    c["PV"].done(ins)
                return run

            def back(b, q):
                c["U"].wait(eng, b + 1)
                c["kz"].wait(eng, upto_b(b + 3))
                c["v"].wait(eng, upto_b(b + 3))
                for g in range(GROUPS):
                    ins = eng.transpose(m_b[:, g * P:g * P + P], uT[:, g, :], ident[:, :])
                c["OT"].done(ins)

            def heads(b, q):
                c["on"].wait(eng, b + 1)
                c["xn2T_e"].wait(eng, b - 1)
                c["pos_e"].wait(eng, b - 3)
                c["x2"].wait(eng, b)
                c["onT"].done(eng.transpose(m_c[:, 0:P], on[:, :], ident[:, :]))

            def out_proj(b, q):
                c["onT_e"].wait(eng, b + 1)
                c["O"].done(eng.matmul(m_c[:, 0:D], onT[:, :], wo_s[:, :], start=True, stop=True))

            def normed(b, q):
                c["xn2"].wait(eng, b + 1)
                c["x2"].wait(eng, upto_b(b + 2))
                c["xn2T_e"].wait(eng, b)
                c["pos_e"].wait(eng, b - 2)
                c["xn2T"].done(eng.transpose(m_c[:, 0:P], xn2[:, q, :], ident[:, :]))

            def router(b, q):
                c["xn2T_e"].wait(eng, b + 1)
                c["ln1T_e"].wait(eng, upto_b(b + 7))
                c["ex"].wait(eng, b)
                c["logits"].done(eng.matmul(m_a[:, 0:E], xn2T[:, :], gate_s[:, :], start=True, stop=True))

            def ranks(b, q):
                c["chosen"].wait(eng, b + 1)
                c["x2"].wait(eng, upto_b(b + 4))
                c["xn2T_e"].wait(eng, upto_b(b + 2))
                c["pos_e"].wait(eng, b)
                for n, over in enumerate((before, ones)):
                    for k in range(2):
                        ins = eng.matmul(m_c[:, P + n * E:P + n * E + E], over[:, :], chosen[:, q % 2, k, :],
                                         start=(k == 0), stop=(k == 1))
                c["pos"].done(ins)

            batches(eng, [(g - 1, scores(g)) for g in range(4)] +
                    [(-3, project), (-6, inputs), (7, back), (9, heads), (10, out_proj), (24, ranks),
                     (16, normed), (19, router)] +
                    [(g + 1, turn(g)) for g in range(4)] + [(g + 2, mix(g)) for g in range(4)])

            ended.wait(eng, 1)
            keep_clock_up(30)
            table.wait(eng, 3)
            ffn_weights.wait(eng, N_FFN)
            weights_l.wait(eng, len(PARTS))
            old = [eng.alloc_register(f"old_expert{n}") for n in range(4)]
            now = [eng.alloc_register(f"expert{n}") for n in range(4)]

            def expert(q, group):
                own = eng.alloc_register(f"tile_expert{next(names)}")
                eng.reg_mov(own, group[q])
                return bass.RuntimeValue.of_register_unchecked(own).with_bounds(min_val=0, max_val=E - 1)

            def tokens(t, q):
                tile_in[q].landed(eng, t, q)
                f["xT_l"].wait(eng, t)
                f["xT"].done(eng.transpose(xT_b[:, 0:P], xs[:, q, 0:D], ident[:, :]))

            def up(t, q):
                h = q % 2
                f["xT_l"].wait(eng, t + 1)
                f["hid"].wait(eng, t - 1)
                e = expert(q, now)
                tok = xsT_h[:, q, :], xsT_l[:, q, :]
                cols = bass.ds(e * HID, HID)
                three_passes(eng, h1_b[h][:, 0:HID], tok, (w1_h[:, cols], w1_l[:, cols]))
                f["h"].done(three_passes(eng, h3_b[h][:, 0:HID], tok, (w3_h[:, cols], w3_l[:, cols])))

            def turn_hidden(t, q):
                h = q % 2
                f["hid"].wait(eng, t + 1)
                f["hT_e"].wait(eng, t - 1)
                for k in range(HC):
                    ins = eng.transpose(hT_b[h][0:CHUNK[k], k * P:k * P + P],
                                        hid[:, h, k * P:k * P + CHUNK[k]], ident[:, :])
                f["hT"].done(ins)

            def down(t, q):
                h = q % 2
                f["hT_e"].wait(eng, t + 1)
                f["y_e"].wait(eng, t)
                e = expert(q, now if q < 2 else old)
                for k in range(HC):
                    ins = eng.matmul(y_b[:, 0:D], hidT[0:CHUNK[k], h, k, :],
                                     w2_s[0:CHUNK[k], k, bass.ds(e * D, D)],
                                     start=(k == 0), stop=(k == HC - 1))
                f["y"].done(ins)

            def experts(t, q):
                if q == 0:
                    eng.load(old + now, t_exp[0:1, bass.ds(t, 8)])

            tiles(eng, [(0, experts), (0, up), (1, turn_hidden), (-2, tokens), (2, down)])


def kernel(**inputs):
    import numpy as np
    import concourse.bacc as bacc
    from concourse.bass_utils import run_bass_kernel_spmd

    p = "L0_xattn_"
    laid = {
        "x": inputs["x"], "ctx_in": inputs["ctx_1024"],
        "wqT": inputs[p + "wq"].T, "bq": inputs[p + "bq"], "wkT": inputs[p + "wk"].T, "bk": inputs[p + "bk"],
        "wvT": inputs[p + "wv"].T, "bv": inputs[p + "bv"], "woT": inputs[p + "wo"].T, "bo": inputs[p + "bo"],
        "gateT": inputs["L0_ffn_gate_w"].T, "ebias": inputs["L0_ffn_expert_bias"],
        "w1": inputs["L0_ffn_w1"], "w2": inputs["L0_ffn_w2"], "w3": inputs["L0_ffn_w3"],
    }
    nc = bacc.Bacc("TRN2", target_bir_lowering=False, num_devices=1)
    arrays, args = {}, {}
    for name, value in laid.items():
        a = np.ascontiguousarray(value)
        arrays[f"in_{name}"] = a
        args[name] = nc.dram_tensor(f"in_{name}", a.shape, mybir.dt.from_np(a.dtype), kind="ExternalInput").ap()
    out = nc.dram_tensor("out_0", laid["x"].shape, F32, kind="ExternalOutput").ap()
    build(nc, out=out, **args)
    r = run_bass_kernel_spmd(nc, [arrays], core_ids=[0])
    return r.results[0]["out_0"]
```

```python
from contextlib import ExitStack

import concourse.bass as bass
from concourse import mybir

F32 = mybir.dt.float32
F32R = mybir.dt.float32r
BF16 = mybir.dt.bfloat16
I32 = mybir.dt.int32
U32 = mybir.dt.uint32
ALU = mybir.AluOpType
ACT = mybir.ActivationFunctionType
AX = mybir.AxisListType

P = 128
HEADS = 16
EPS = 1e-5


class Counter:

    def __init__(self, sem, step=1):
        self.sem, self.step = sem, step

    def done(self, ins):
        ins.then_inc(self.sem, self.step)

    def wait(self, eng, runs):
        if isinstance(runs, int) and runs <= 0:
            return
        eng.wait_ge(self.sem, runs * self.step)


class Ring(Counter):

    def __init__(self, sem, n, per=1):
        super().__init__(sem, 16)
        self.n, self.per = n, per

    def landed(self, eng, item, q):
        eng.wait_ge(self.sem, (item - q) * (16 * self.per // self.n) + 16 * self.per)

    def reusable(self, eng, item, q):
        if not (isinstance(item, int) and item < self.n):
            eng.wait_ge(self.sem, (item - q) * (16 * self.per // self.n))


def walk(eng, steps, per, unroll, first, last, low, high, total):

    def one(rnd, phase):
        for g in range(per):
            for slot, run in steps:
                if (slot - g) % per == 0:
                    back = (slot - g) // per
                    item = rnd - back
                    if isinstance(item, int) and not 0 <= item < total:
                        continue
                    run(item, (phase - back) % unroll)

    for r in range(first, low):
        one(r, r % unroll)
    with eng.Fori(0, (high - low) // unroll) as r:
        for u in range(unroll):
            one(r * unroll + (low + u), (low + u) % unroll)
    for r in range(high, last + 1):
        one(r, r % unroll)


def build(nc, x, ctx_in, wqT, bq, wkT, bk, wvT, bv, woT, bo, gateT, ebias, w1, w2, w3, out):
    B, S, D = x.shape
    K = ctx_in.shape[1]
    DH = D // HEADS
    E, _, HID = w1.shape
    T = B * S
    SCALE = float(DH) ** -0.5
    GROUPS = 4
    HC = (HID + P - 1) // P
    CHUNK = [min(P, HID - c * P) for c in range(HC)]
    CAP = T + P
    NT = 2 * T // P + E - 1
    SPARE = (E - 1) * P
    ROW = D + 1
    NOWHERE = 4 * T
    assert S == P and D == P and HEADS == 4 * GROUPS and DH == 8

    xs_dram = nc.dram_tensor("expert_rows", [E * CAP + SPARE, ROW], F32, kind="Internal").ap()
    y_dram = nc.dram_tensor("expert_results", [2 * T, D], F32, kind="Internal").ap()

    with ExitStack() as stack:
        def sb(name, shape, dt=F32):
            return stack.enter_context(nc.sbuf_tensor(name, shape, dt))

        def ps(name, shape, dt=F32):
            return stack.enter_context(nc.psum_tensor(name, shape, dt))

        names = iter(range(10 ** 6))

        def counter(name, step=1):
            return Counter(stack.enter_context(nc.semaphore(f"{name}_{next(names)}")), step)

        def ring(name, n, per=1):
            return Ring(stack.enter_context(nc.semaphore(name)), n, per)

        wq_s, wk_s, wv_s, wo_s = (sb(n, [P, D]) for n in ("wq_s", "wk_s", "wv_s", "wo_s"))
        gate_s = sb("gate_s", [P, E])
        bq_s, bk_s, bqs_s = sb("bq_s", [P, 1]), sb("bk_s", [P, 1]), sb("bqs_s", [P, 1])
        bv_s, bo_b, bo_sum, eb_b = sb("bv_s", [P, 1]), sb("bo_b", [P, D]), sb("bo_sum", [P, D]), sb("eb_b", [P, E])
        w1_s, w3_s = sb("w1_s", [P, E * HID]), sb("w3_s", [P, E * HID])
        w2_s = sb("w2_s", [P, HC, E * D])
        w1_h, w1_l = sb("w1_h", [P, E * HID], F32R), sb("w1_l", [P, E * HID], F32R)
        w3_h, w3_l = sb("w3_h", [P, E * HID], F32R), sb("w3_l", [P, E * HID], F32R)
        ident = sb("ident", [P, P])
        head1, headmask = sb("head1", [P, HEADS]), sb("headmask", [P, 4])
        before = sb("before", [P, P], BF16)
        ones = sb("ones", [P, P], BF16)
        iota_e = sb("iota_e", [P, E])
        minus_half = sb("minus_half", [P, 1])
        place_of = sb("place_of", [P, B, 2], I32)
        XB = 4
        x_s, c_s = sb("x_s", [P, XB, D]), sb("c_s", [P, XB, D])
        x2 = sb("x2", [P, B, D])
        st1, mv1, ve1 = sb("st1", [P, 6]), sb("mv1", [P, 2, 2]), sb("ve1", [P, 2])
        rs1, sh1 = sb("rs1", [P, 2]), sb("sh1", [P, 2])
        st2, mv2, ve2 = sb("st2", [P, 6]), sb("mv2", [P, 2, 2]), sb("ve2", [P, 2])
        rs2, sh2 = sb("rs2", [P, 2]), sb("sh2", [P, 2])
        xn = sb("xn", [P, 2, D])
        xcT = sb("xcT", [P, D + K])
        qT_h, qT_l = sb("qT_h", [P, 4, P], F32R), sb("qT_l", [P, 4, P], F32R)
        kT_h, kT_l = sb("kT_h", [P, 2, K], F32R), sb("kT_l", [P, K], F32R)
        kz_h, kz_l = sb("kz_h", [P, 2, 4, K], F32R), sb("kz_l", [P, 2, 4, K], F32R)
        v1 = sb("v1", [P, 4, HEADS, DH + 1])
        nmx = sb("nmx", [P, 2, 4])
        prob = sb("prob", [P, GROUPS, 4, K])
        pT = sb("pT", [P, GROUPS, 4, P])
        uT = sb("uT", [P, GROUPS, P])
        rden, on, onT = sb("rden", [P, HEADS]), sb("on", [P, D]), sb("onT", [P, P])
        x2s = sb("x2s", [P, 2, D])
        xn2, xn2T = sb("xn2", [P, 4, D]), sb("xn2T", [P, P])
        lmax, ex, esum = sb("lmax", [P, 1]), sb("ex", [P, 2, E]), sb("esum", [P, 2])
        rsum, biased = sb("rsum", [P, 2]), sb("biased", [P, E])
        top, topi = sb("top", [P, 8]), sb("topi", [P, 8], U32)
        chosen = sb("chosen", [P, 2, 2, E], BF16)
        gate_w, gates = sb("gate_w", [P, 2, E]), sb("gates", [P, 2, 2])
        pos = sb("pos", [P, 2, E])
        row_of = sb("row_of", [P, 2, 2, E])
        place_w, places = sb("place_w", [P, 2, E]), sb("places", [P, 2, 2], I32)
        rows = sb("rows", [P, 2, 2, ROW])
        region_less = sb("region_less", [1, E])
        upto_e = sb("upto_e", [1, E, E])
        cnt, ntile, jump = sb("cnt", [1, E], I32), sb("ntile", [1, E], I32), sb("jump", [1, E])
        part, upto = sb("part", [1, E, E]), sb("upto", [1, E])
        tvec, passed, skip = sb("tvec", [1, NT]), sb("passed", [1, NT]), sb("skip", [1, NT])
        passes = w1_s[0:1, 0:NT * E].rearrange("p (t e) -> p t e", e=E)
        skips = w1_s[0:1, NT * E:2 * NT * E].rearrange("p (t e) -> p t e", e=E)
        ends = sb("ends", [1, E], I32)
        t_exp, t_row = sb("t_exp", [1, 4 + (NT + 3) // 4 * 4], I32), sb("t_row", [1, NT], I32)
        padding = sb("padding", [P, ROW])
        xs = sb("xs", [P, 4, ROW])
        where = sb("where", [P, 4], I32)
        xsT_h, xsT_l = sb("xsT_h", [P, 4, P], F32R), sb("xsT_l", [P, 4, P], F32R)
        act, hid = sb("act", [P, 2, HID]), sb("hid", [P, 2, HID])
        hidT = sb("hidT", [P, 2, HC, P])
        y_s = sb("y_s", [P, 4, D])
        LG, YB = 4, 4
        both, tot = sb("both", [P, YB, LG, 2, D]), sb("tot", [P, YB, LG, D])

        bank = [ps(f"bank{n}", [P, 512]) for n in range(8)]
        score_b, prT_b, u_b, m_a, m_b, m_c = bank[0:2], bank[2:4], bank[4], bank[5], bank[6], bank[7]
        h1_b, h3_b, hT_b, y_b, xT_b = bank[0:2], bank[2:4], bank[4:6], bank[6], bank[7]

        weights, ffn_weights, consts = counter("weights", 16), counter("ffn_weights", 16), counter("consts")
        mask_r, ready, bo_p, bo_ready = (counter(n) for n in ("mask_r", "ready", "bo_p", "bo_ready"))
        spare_r = counter("spare_r", 16)
        weights_h, weights_l = counter("weights_h"), counter("weights_l")
        c = {n: counter(n) for n in (
            "stats1 var1 eps1 rstd1 shift1 xn xbo ln1T ln1T_e proj qT qT_l kT kT_l kz_h kz_l v S max sub exp "
            "PT PT_e PV U OT rden on onT onT_e O x2 keep stats2 var2 eps2 rstd2 shift2 xn2 xn2T xn2T_e "
            "logits lmax ex rsum biased top topi chosen gate_w gates pos pos_e row_of place_w places "
            "rows1 rows2 placed").split()}
        loads = [ring(f"loads{n}", XB, 2) for n in range(XB)]
        scat = [ring(f"scat{n}", 2, 2) for n in range(2)]
        table, ended, padded = counter("table"), counter("ended"), counter("padded", 16)
        pad_rows = counter("pad_rows")
        f = {n: counter("f_" + n) for n in "xT xT_h xT_l where h act hid hT hT_e y y_e".split()}
        tile_in = [ring(f"tile_in{n}", 4) for n in range(4)]
        tile_out = [ring(f"tile_out{n}", 4) for n in range(4)]
        y_in = [ring(f"y_in{n}", YB) for n in range(YB)]
        added, total, stored = counter("added"), counter("total"), [ring(f"stored{n}", YB) for n in range(YB)]
        block = stack.enter_context(nc.Block())

        N_WEIGHTS, N_FFN, N_CONSTS = 10, 2 + HC, 18

        def batches(eng, steps):
            walk(eng, steps, GROUPS, 4, -5, B + 5, 8, B - 8, B)

        def tiles(eng, steps):
            walk(eng, steps, 1, 4, -2, NT + 1, 6, 6 + (NT - 8) // 4 * 4, NT)

        PARTS = [tuple(w[:, n * HID * E // 2:(n + 1) * HID * E // 2] for w in ws)
                 for ws in ((w1_s, w1_h, w1_l), (w3_s, w3_h, w3_l)) for n in range(2)]
        SPLIT_AT = [2, 3, 4, 5]

        def three_passes(eng, out, lhs, rhs, **where):
            (lh, ll), (rh, rl) = lhs, rhs
            eng.matmul(out, lh, rh, start=True, stop=False, **where)
            eng.matmul(out, lh, rl, start=False, stop=False, **where)
            return eng.matmul(out, ll, rh, start=False, stop=True, **where)

        def late(b):
            return isinstance(b, int) and b >= B - 5

        BY_HEAD = (2,)

        def sub_runs(b, g):
            return (4 - len(BY_HEAD)) * b + sum(j not in BY_HEAD for j in range(g + 1))

        def scores_out(eng, b, g):
            if (g - 2) % 4 in BY_HEAD:
                c["exp"].wait(eng, 4 * b + g - 1)
            else:
                c["sub"].wait(eng, sub_runs(b - (g < 2), (g - 2) % 4))

        def settled(eng):
            eng.nop(nofuse=True)

        def upto_b(n):
            return min(n, B) if isinstance(n, int) else n

        @block.sync
        def _(eng):
            for dst, src in ((wq_s, wqT), (wk_s, wkT), (wv_s, wvT), (wo_s, woT), (gate_s, gateT)):
                weights.done(eng.dma_start(dst[:, :], src))
            for dst, src in ((bq_s, bq), (bk_s, bk), (bv_s, bv)):
                weights.done(eng.dma_start(dst[:, :], src.rearrange("(p a) -> p a", a=1)))
            for dst, src in ((bo_b, bo), (eb_b, ebias)):
                n = src.shape[0]
                weights.done(eng.dma_start(dst[:, :], src.rearrange("(a n) -> a n", a=1).broadcast_to((P, n))))

            def load(b, q):
                for step in ("xn", "xbo", "ln1T"):
                    c[step].wait(eng, b - XB + 1)
                loads[q].done(eng.dma_start(x_s[:, q, :], x[bass.ds(b, 1), :, :].rearrange("a s d -> (a s) d")))
                loads[q].done(eng.dma_start(c_s[0:K, q, :],
                                            ctx_in[bass.ds(b, 1), :, :].rearrange("a s d -> (a s) d")))

            for b in range(XB):
                load(b, b)
            for dst, src in ((w1_s, w1), (w3_s, w3)):
                ffn_weights.done(eng.dma_start(dst[:, :].rearrange("p (e h) -> p e h", e=E),
                                               src.rearrange("e p h -> p e h")))
            for h in range(HC):
                ffn_weights.done(eng.dma_start(
                    w2_s[0:CHUNK[h], h, :].rearrange("p (e n) -> p e n", e=E),
                    w2[:, h * P:h * P + CHUNK[h], :].rearrange("e p n -> p e n")))
            pad_rows.wait(eng, 2)
            for n in range(E - 1):
                r = E * CAP + n * P
                spare_r.done(eng.dma_start(xs_dram[r:r + P, :], padding[:, :]))
            with eng.Fori(1, B // XB) as r:
                for q in range(XB):
                    load(r * XB + q, q)

            ended.wait(eng, 1)
            end_rows = [eng.alloc_register(f"end_row{e}") for e in range(E)]
            eng.load(end_rows, ends[0:1, :])
            for reg in end_rows:
                row = bass.RuntimeValue.of_register_unchecked(reg).with_bounds(min_val=0, max_val=E * CAP - P)
                padded.done(eng.dma_start(xs_dram[bass.ds(row, P), :], padding[:, :]))

            for n in range(2):
                scat[n].wait(eng, B)
            padded.wait(eng, E)
            spare_r.wait(eng, E - 1)
            table.wait(eng, 1)

            def tile_load(t, q):
                f["xT"].wait(eng, t - 3)
                f["where"].wait(eng, t - 3)
                row = eng.value_load(t_row[0:1, bass.ds(t, 1)], min_val=0, max_val=E * CAP + SPARE - P)
                tile_in[q].done(eng.dma_start(xs[:, q, :], xs_dram[bass.ds(row, P), :]))

            for t in range(4):
                tile_load(t, t)
            last = NT // 4 * 4
            with eng.Fori(1, last // 4) as r:
                for q in range(4):
                    tile_load(r * 4 + q, q)
            for t in range(last, NT):
                tile_load(t, t % 4)

            for q in range(4):
                tile_out[q].wait(eng, (NT - q + 3) // 4)

            def y_load(n, q):
                added.wait(eng, n - YB + 1)
                src = y_dram.rearrange("(p b k) d -> p b k d", p=P, k=2)[:, bass.ds(n * LG, LG), :, :]
                y_in[q].done(eng.dma_start(both[:, q, :, :, :], src))

            for n in range(YB):
                y_load(n, n)
            with eng.Fori(1, B // LG // YB) as r:
                for q in range(YB):
                    y_load(r * YB + q, q)

        @block.gpsimd
        def _(eng):
            pad_rows.done(eng.memset(padding[:, 0:D], 0.0))
            pad_rows.done(eng.memset(padding[:, D:ROW].bitcast(I32), NOWHERE))
            made = [0]

            def const(ins):
                consts.done(ins)
                made[0] += 1
                consts.wait(eng, made[0])

            const(eng.memset(minus_half[:, :], -0.5))
            const(eng.memset(ident[:, :], 0.0))
            const(eng.affine_select(out=ident[:, :], in_=ident[:, :], compare_op=ALU.not_equal, fill=1.0,
                                    base=0, pattern=[[-1, P]], channel_multiplier=1))
            const(eng.memset(head1[:, :], 1.0))
            const(eng.affine_select(out=head1[:, :], in_=head1[:, :], compare_op=ALU.is_ge, fill=0.0,
                                    base=0, pattern=[[-DH, HEADS]], channel_multiplier=1))
            const(eng.affine_select(out=head1[:, :], in_=head1[:, :], compare_op=ALU.is_ge, fill=0.0,
                                    base=DH - 1, pattern=[[DH, HEADS]], channel_multiplier=-1))
            const(eng.memset(before[:, :], 1.0))
            const(eng.affine_select(out=before[:, :], in_=before[:, :], compare_op=ALU.is_gt, fill=0.0,
                                    base=0, pattern=[[1, P]], channel_multiplier=-1))
            const(eng.memset(ones[:, :], 1.0))
            const(eng.iota(iota_e[:, :], [[1, E]], base=0, channel_multiplier=0,
                           allow_small_or_imprecise_dtypes=True))
            const(eng.iota(region_less[:, :], [[CAP, E]], base=1 - P, channel_multiplier=0,
                           allow_small_or_imprecise_dtypes=True))
            const(eng.memset(upto_e[:, :, :], 1.0))
            const(eng.affine_select(out=upto_e[:, :, :], in_=upto_e[:, :, :], compare_op=ALU.is_ge, fill=0.0,
                                    base=0, pattern=[[1, E], [-1, E]], channel_multiplier=0))
            const(eng.iota(row_of[:, 1, 1, :], [[CAP, E]], base=0, channel_multiplier=0,
                           allow_small_or_imprecise_dtypes=True))
            const(eng.iota(place_of[:, :, :], [[2, B], [1, 2]], base=0, channel_multiplier=2 * B))
            const(eng.iota(tvec[:, :], [[1, NT]], base=0, channel_multiplier=0,
                           allow_small_or_imprecise_dtypes=True))
            const(eng.memset(v1[:, :, :, :], 1.0))
            const(eng.memset(xcT[:, :], 0.0))
            assert made[0] == N_CONSTS
            weights.wait(eng, N_WEIGHTS)

            def rstd(n, mv, ve, rs, sh):
                def run(b, q):
                    h = q % 2
                    c[f"var{n}"].wait(eng, b + 1)
                    c["xn" if n == 1 else "xn2"].wait(eng, b - 1)
                    settled(eng)
                    c[f"eps{n}"].done(eng.tensor_scalar(ve[:, h:h + 1], mv[:, h, 1:2], EPS, None, ALU.add))
                    c[f"eps{n}"].wait(eng, b + 1)
                    c[f"rstd{n}"].done(eng.tensor_tensor(rs[:, h:h + 1], ve[:, h:h + 1], minus_half[:, :],
                                                         ALU.pow))
                    c[f"rstd{n}"].wait(eng, b + 1)
                    settled(eng)
                    c[f"shift{n}"].done(eng.tensor_scalar(sh[:, h:h + 1], mv[:, h, 0:1], rs[:, h:h + 1], -1.0,
                                                          ALU.mult, ALU.mult))
                return run

            def keep_input(b, q):
                loads[q].landed(eng, b, q)
                c["xbo"].done(eng.tensor_tensor(x2[:, bass.ds(b, 1), :].rearrange("p a d -> p (a d)"),
                                                x_s[:, q, :], bo_sum[:, :], ALU.add))

            def keep(b, q):
                if late(b):
                    return
                c["x2"].wait(eng, b + 1)
                settled(eng)
                c["keep"].done(eng.tensor_copy(x2[:, bass.ds(b, 1), :].rearrange("p a d -> p (a d)"),
                                               x2s[:, q % 2, :]))

            def scatter(b, q):
                h = q % 2
                scat[h].reusable(eng, b, h)
                c["gates"].wait(eng, b + 1)
                c["xn2"].wait(eng, b + 1)
                settled(eng)
                for k in range(0 if late(b) else 2):
                    c[f"rows{k + 1}"].done(eng.tensor_scalar(rows[:, h, k, 0:D], xn2[:, q, :],
                                                             gates[:, h, k:k + 1], rsum[:, h:h + 1],
                                                             ALU.mult, ALU.mult))
                c["placed"].done(eng.tensor_copy(
                    rows[:, h, :, D:ROW].bitcast(I32),
                    place_of[:, bass.ds(b, 1), :].rearrange("p a k -> p k a")))
                for k in range(2):
                    c[f"rows{k + 1}"].wait(eng, b + 1)
                c["placed"].wait(eng, b + 1)
                c["places"].wait(eng, b + 1)
                settled(eng)
                for k in range(2):
                    scat[h].done(eng.indirect_dma_start(
                        xs_dram, bass.IndirectOffsetOnAxis(ap=places[:, h, k:k + 1], axis=0),
                        rows[:, h, k, :], None))

            bo_ready.wait(eng, 1)
            batches(eng, [(-14, rstd(1, mv1, ve1, rs1, sh1)), (12, rstd(2, mv2, ve2, rs2, sh2)), (13, keep),
                          (-15, keep_input), (27, scatter)])

            def keep_places(t, q):
                tile_in[q].landed(eng, t, q)
                tile_out[q].reusable(eng, t, q)
                settled(eng)
                f["where"].done(eng.tensor_copy(where[:, q:q + 1], xs[:, q, D:ROW].bitcast(I32)))

            def results(t, q):
                f["y_e"].wait(eng, t + 1)
                f["where"].wait(eng, t + 1)
                settled(eng)
                tile_out[q].done(eng.indirect_dma_start(
                    y_dram, bass.IndirectOffsetOnAxis(ap=where[:, q:q + 1], axis=0), y_s[:, q, :], None,
                    bounds_check=2 * T - 1, oob_is_err=False))

            tiles(eng, [(2, results), (-1, keep_places)])

        @block.vector
        def _(eng):
            consts.wait(eng, N_CONSTS)
            weights.wait(eng, N_WEIGHTS)
            mask_r.done(eng.tensor_reduce(headmask[:, :], head1[:, :].rearrange("p (g j) -> p j g", j=4),
                                          AX.X, ALU.add))
            mask_r.wait(eng, 1)
            ready.done(eng.tensor_scalar(wq_s[:, :], wq_s[:, :], SCALE, None, ALU.mult))
            ready.done(eng.tensor_scalar(bqs_s[:, :], bq_s[:, :], SCALE, None, ALU.mult))
            ready.done(eng.memset(u_b[:, :], 0.0))

            bo_p.wait(eng, 1)
            bo_ready.done(eng.tensor_tensor(bo_sum[:, :], bo_b[:, :], m_c[:, 0:D], ALU.add))

            def stats1(b, q):
                loads[q].landed(eng, b, q)
                c["var1"].wait(eng, b)
                settled(eng)
                c["stats1"].done(eng.bn_stats(st1[:, :], x_s[:, q, :]))

            def var1(b, q):
                c["stats1"].wait(eng, b + 1)
                c["xn"].wait(eng, b - 1)
                settled(eng)
                c["var1"].done(eng.bn_aggr(mv1[:, q % 2, :], st1[:, :]))

            def low_parts_qk(b, q):
                h = q % 2
                c["kT"].wait(eng, b + 1)
                c["S"].wait(eng, 4 * b - 12)
                c["qT_l"].done(eng.scalar_tensor_tensor(out=qT_l[:, q, :], in0=m_a[:, 0:P], scalar=bqs_s[:, 0:1],
                                                        in1=qT_h[:, q, :], op0=ALU.add, op1=ALU.subtract))
                c["kz_l"].wait(eng, b)
                c["kT_l"].done(eng.scalar_tensor_tensor(out=kT_l[:, :], in0=m_b[:, 0:K], scalar=bk_s[:, 0:1],
                                                        in1=kT_h[:, h, :], op0=ALU.add, op1=ALU.subtract))

            def high_keys(b, q):
                h = q % 2
                c["kT"].wait(eng, b + 1)
                c["S"].wait(eng, 4 * b - 4)
                c["kz_h"].done(eng.tensor_tensor(kz_h[:, h, :, :],
                                                 kT_h[:, h, :].unsqueeze(1).broadcast_to((P, 4, K)),
                                                 headmask[:, :].unsqueeze(2).broadcast_to((P, 4, K)), ALU.mult))

            def low_keys(b, q):
                h = q % 2
                c["kT_l"].wait(eng, b + 1)
                c["kz_l"].done(eng.tensor_tensor(kz_l[:, h, :, :],
                                                 kT_l[:, :].unsqueeze(1).broadcast_to((P, 4, K)),
                                                 headmask[:, :].unsqueeze(2).broadcast_to((P, 4, K)), ALU.mult))

            def maxima(g):
                def run(b, q):
                    n, h = 4 * b + g, g % 2
                    c["S"].wait(eng, n + 1)
                    scores_out(eng, b, g)
                    c["max"].done(eng.tensor_reduce(nmx[:, h, :], score_b[h][:, 0:4 * K].rearrange(
                        "p (j k) -> p j k", j=4), AX.X, ALU.max, negate=True))
                return run

            def shifted(g):
                def run(b, q):
                    n, h = 4 * b + g, g % 2
                    c["max"].wait(eng, n + 1)
                    c["PT"].wait(eng, n - 3)
                    c["sub"].done(eng.tensor_tensor(
                        prob[:, g, :, :], score_b[h][:, 0:4 * K].rearrange("p (j k) -> p j k", j=4),
                        nmx[:, h, :].unsqueeze(2).broadcast_to((P, 4, K)), ALU.add))
                return run

            def denominators(b, q):
                c["OT"].wait(eng, b + 1)
                c["on"].wait(eng, b)
                c["rden"].done(eng.reciprocal(rden[:, :].unsqueeze(2), o_all[:, :, DH:DH + 1]))

            def divide(b, q):
                c["rden"].wait(eng, b + 1)
                c["onT"].wait(eng, b)
                c["on"].done(eng.tensor_tensor(on[:, :].rearrange("p (n d) -> p n d", d=DH), o_all[:, :, 0:DH],
                                               rden[:, :].unsqueeze(2).broadcast_to((P, HEADS, DH)), ALU.mult))

            def residual(b, q):
                c["O"].wait(eng, b + 1)
                c["xbo"].wait(eng, b + 1)
                c["keep"].wait(eng, b - 1)
                c["xn2"].wait(eng, b - 1)
                c["x2"].done(eng.tensor_tensor(x2s[:, q % 2, :], m_c[:, 0:D],
                                               x2[:, bass.ds(b, 1), :].rearrange("p a d -> p (a d)"), ALU.add))

            def stats2(b, q):
                c["x2"].wait(eng, b + 1)
                c["var2"].wait(eng, b)
                settled(eng)
                c["stats2"].done(eng.bn_stats(st2[:, :], x2s[:, q % 2, :]))

            def var2(b, q):
                c["stats2"].wait(eng, b + 1)
                c["xn2"].wait(eng, b - 1)
                settled(eng)
                c["var2"].done(eng.bn_aggr(mv2[:, q % 2, :], st2[:, :]))

            def logit_max(b, q):
                c["logits"].wait(eng, b + 1)
                c["ex"].wait(eng, b)
                c["lmax"].done(eng.tensor_reduce(lmax[:, :], m_a[:, 0:E], AX.X, ALU.max, negate=True))

            def share(b, q):
                h = q % 2
                c["ex"].wait(eng, b + 1)
                c["rows2"].wait(eng, b - 1)
                c["rsum"].done(eng.reciprocal(rsum[:, h:h + 1], esum[:, h:h + 1]))

            def bias(b, q):
                h = q % 2
                c["rsum"].wait(eng, b + 1)
                c["topi"].wait(eng, b)
                c["biased"].done(eng.scalar_tensor_tensor(out=biased[:, :], in0=ex[:, h, :],
                                                          scalar=rsum[:, h:h + 1], in1=eb_b[:, :],
                                                          op0=ALU.mult, op1=ALU.add))

            def best(b, q):
                c["biased"].wait(eng, b + 1)
                c["topi"].wait(eng, b)
                settled(eng)
                c["top"].done(eng.max(top[:, :], biased[:, :]))

            def best_index(b, q):
                c["top"].wait(eng, b + 1)
                c["chosen"].wait(eng, b)
                settled(eng)
                c["topi"].done(eng.max_index(topi[:, :], top[:, :], biased[:, :]))

            def one_hot(b, q):
                c["topi"].wait(eng, b + 1)
                c["pos"].wait(eng, b - 1)
                c["place_w"].wait(eng, b - 1)
                c["chosen"].done(eng.tensor_tensor(
                    chosen[:, q % 2, :, :], iota_e[:, :].unsqueeze(1).broadcast_to((P, 2, E)),
                    topi[:, 0:2].unsqueeze(2).broadcast_to((P, 2, E)), ALU.is_equal))

            def gate_parts(b, q):
                h = q % 2
                c["chosen"].wait(eng, b + 1)
                c["gates"].wait(eng, b)
                c["gate_w"].done(eng.tensor_tensor(gate_w[:, :, :], chosen[:, h, :, :],
                                                   ex[:, h, :].unsqueeze(1).broadcast_to((P, 2, E)), ALU.mult))

            def gate_sums(b, q):
                c["gate_w"].wait(eng, b + 1)
                c["rows2"].wait(eng, b - 1)
                c["gates"].done(eng.tensor_reduce(gates[:, q % 2, :], gate_w[:, :, :], AX.X, ALU.add))

            def rank(b, q):
                h = q % 2
                c["pos_e"].wait(eng, b + 1)
                c["row_of"].wait(eng, b)
                c["place_w"].wait(eng, b - 1)
                c["row_of"].done(eng.tensor_tensor(
                    row_of[:, h, :, :], pos[:, :, :],
                    row_of[:, 1 - h, 1, :].unsqueeze(1).broadcast_to((P, 2, E)), ALU.add))

            def place_parts(b, q):
                h = q % 2
                c["row_of"].wait(eng, b + 1)
                c["places"].wait(eng, b)
                c["place_w"].done(eng.tensor_tensor(
                    place_w[:, :, :], chosen[:, h, :, :],
                    row_of[:, h, 0, :].unsqueeze(1).broadcast_to((P, 2, E)), ALU.mult))

            def place_sums(b, q):
                h = q % 2
                c["place_w"].wait(eng, b + 1)
                scat[h].reusable(eng, b, h)
                with nc.allow_low_precision(reason="row numbers are whole and below 2**24"):
                    c["places"].done(eng.tensor_reduce(places[:, h, :], place_w[:, :, :], AX.X, ALU.add))

            def late_rows(b, q):
                if late(b):
                    h = q % 2
                    scat[h].reusable(eng, b, h)
                    c["gates"].wait(eng, b + 1)
                    c["rsum"].wait(eng, b + 1)
                    c["xn2"].wait(eng, b + 1)
                    for k in range(2):
                        c[f"rows{k + 1}"].wait(eng, b)
                        c[f"rows{k + 1}"].done(eng.tensor_scalar(rows[:, h, k, 0:D], xn2[:, q, :],
                                                                 gates[:, h, k:k + 1], rsum[:, h:h + 1],
                                                                 ALU.mult, ALU.mult))

            def low_parts(b, q):
                if isinstance(b, int) and b in SPLIT_AT:
                    n = SPLIT_AT.index(b)
                    whole, high, low = PARTS[n]
                    weights_h.wait(eng, n + 1)
                    weights_l.done(eng.tensor_tensor(low, whole, high, ALU.subtract))

            o_all = m_b[:, :].rearrange("p (n w) -> p n w", w=32)
            batches(eng, [(g, maxima(g)) for g in range(4)] +
                    [(-17, stats1), (11, residual), (12, var2), (20, logit_max), (22, bias), (23, best_index),
                     (24, gate_parts), (26, rank), (27, place_sums), (8, denominators),
                     (-6, low_parts_qk)] +
                    [(g, shifted(g)) for g in range(4) if g not in BY_HEAD] +
                    [(-15, var1), (-5, high_keys), (-3, low_keys), (8, divide), (11, stats2), (21, share), (22, best),
                     (23, one_hot), (24, gate_sums), (26, place_parts), (25, late_rows), (3, low_parts)])

            made = [0]

            def link(ins):
                c["row_of"].done(ins)
                made[0] += 1
                c["row_of"].wait(eng, B + made[0])

            def sums(out, parts):
                link(eng.tensor_reduce(out, parts, AX.X, ALU.add))

            c["row_of"].wait(eng, B)
            c["keep"].wait(eng, B)
            final = row_of[0:1, (B - 1) % 2, 1, :]
            ended.done(eng.tensor_copy(ends[:, :], final))
            link(eng.memset(t_exp[:, :], 0))
            link(eng.tensor_tensor(cnt[:, :], final, region_less[:, :], ALU.subtract))
            link(eng.tensor_scalar(ntile[:, :], cnt[:, :], P.bit_length() - 1, None, ALU.logical_shift_right))
            link(eng.tensor_scalar(jump[:, :], ntile[:, :], -float(P), float(CAP), ALU.mult, ALU.add))
            link(eng.tensor_tensor(part[:, :, :], upto_e[:, :, :],
                                   ntile[:, :].unsqueeze(1).broadcast_to((1, E, E)), ALU.mult))
            sums(upto[:, :], part[:, :, :])
            link(eng.tensor_tensor(passes, tvec[:, :].unsqueeze(2).broadcast_to((1, NT, E)),
                                   upto[:, :].unsqueeze(1).broadcast_to((1, NT, E)), ALU.is_ge))
            link(eng.tensor_tensor(skips, passes, jump[:, :].unsqueeze(1).broadcast_to((1, NT, E)), ALU.mult))
            sums(skip[:, :], skips)
            table.done(eng.scalar_tensor_tensor(out=t_row[:, :], in0=tvec[:, :], scalar=float(P),
                                                in1=skip[:, :], op0=ALU.mult, op1=ALU.add))
            sums(passed[:, :], passes)
            table.done(eng.tensor_scalar(t_exp[:, 4:4 + NT], passed[:, :], float(E - 1), None, ALU.min))
            for b in hT_b:
                table.done(eng.memset(b[:, :], 0.0))

            def gated(t, q):
                h = q % 2
                f["act"].wait(eng, t + 1)
                f["hT"].wait(eng, t - 1)
                f["hid"].done(eng.tensor_tensor(hid[:, h, :], h3_b[h][:, 0:HID], act[:, h, :], ALU.mult))

            def hidden(t, q):
                h = q % 2
                f["hT"].wait(eng, t + 1)
                f["y"].wait(eng, t - 1)
                f["hT_e"].done(eng.tensor_copy(hidT[:, h, :, :],
                                               hT_b[h][:, 0:HC * P].rearrange("p (c t) -> p c t", c=HC)))

            def tokens_low(t, q):
                f["xT_h"].wait(eng, t + 1)
                f["h"].wait(eng, t - 3)
                f["xT_l"].done(eng.tensor_tensor(xsT_l[:, q, :], xT_b[:, 0:P], xsT_h[:, q, :], ALU.subtract))

            tiles(eng, [(1, hidden), (-2, tokens_low), (0, gated)])

            def add_up(n, q):
                y_in[q].landed(eng, n, q)
                stored[q].reusable(eng, n, q)
                added.done(eng.tensor_tensor(tot[:, q, :, :], both[:, q, :, 0, :], both[:, q, :, 1, :], ALU.add))
                added.wait(eng, n + 1)
                total.done(eng.tensor_tensor(tot[:, q, :, :], tot[:, q, :, :],
                                             x2[:, bass.ds(n * LG, LG), :], ALU.add))

            for n in range(YB):
                add_up(n, n)
            with eng.Fori(1, B // LG // YB) as r:
                for q in range(YB):
                    add_up(r * YB + q, q)

        @block.scalar
        def _(eng):
            ready.wait(eng, 3)

            def exps(g):
                def run(b, q):
                    n, h = 4 * b + g, g % 2
                    if g in BY_HEAD:
                        c["max"].wait(eng, n + 1)
                        c["PT"].wait(eng, n - 3)
                        for j in range(4):
                            ins = eng.activation(prob[:, g, j, :], score_b[h][:, j * K:j * K + K], ACT.Exp,
                                                 bias=nmx[:, h, j:j + 1])
                        c["exp"].done(ins)
                    else:
                        c["sub"].wait(eng, sub_runs(b, g))
                        c["exp"].done(eng.activation(prob[:, g, :, :], prob[:, g, :, :], ACT.Exp))
                return run

            def probs(g):
                def run(b, q):
                    n, h = 4 * b + g, g % 2
                    c["PT"].wait(eng, n + 1)
                    c["PV"].wait(eng, n - 3)
                    c["PT_e"].done(eng.activation(pT[0:K, g, :, :],
                                                  prT_b[h][0:K, :].rearrange("k (j t) -> k j t", j=4), ACT.Copy))
                return run

            def inputs(b, q):
                c["ln1T"].wait(eng, b + 1)
                c["proj"].wait(eng, b)
                c["ln1T_e"].done(eng.activation(xcT[:, :], m_a[:, 0:D + K], ACT.Copy))

            def queries(b, q):
                h = q % 2
                c["proj"].wait(eng, b + 1)
                c["S"].wait(eng, 4 * b - 12)
                c["qT"].done(eng.activation(qT_h[:, q, :], m_a[:, 0:P], ACT.Identity, bias=bqs_s[:, 0:1]))
                c["kT_l"].wait(eng, b - 1)
                c["kz_h"].wait(eng, b - 1)
                c["kT"].done(eng.activation(kT_h[:, h, :], m_b[:, 0:K], ACT.Identity, bias=bk_s[:, 0:1]))

            def values(b, q):
                c["kT_l"].wait(eng, b + 1)
                c["PV"].wait(eng, 4 * b - 12)
                c["v"].done(eng.activation(v1[0:K, q, :, 0:DH],
                                           m_b[0:K, P:2 * P].rearrange("p (n d) -> p n d", d=DH), ACT.Copy))

            def normalise(n, src, mv_done, dst_ring, dst):
                def run(b, q):
                    h = q % 2
                    c[f"shift{n}"].wait(eng, b + 1)
                    if n == 1:
                        c["ln1T"].wait(eng, b - 1)
                    else:
                        c["rows2"].wait(eng, b - 3)
                    c[mv_done].done(eng.activation(dst[:, q % dst_ring, :], src(q), ACT.Identity,
                                                   bias=(sh1, sh2)[n - 1][:, h:h + 1],
                                                   scale=(rs1, rs2)[n - 1][:, h:h + 1]))
                return run

            def late_keep(b, q):
                if late(b):
                    c["x2"].wait(eng, b + 1)
                    c["keep"].wait(eng, b)
                    c["keep"].done(eng.activation(x2[:, b, :], x2s[:, q % 2, :], ACT.Copy))

            def high_parts(b, q):
                if isinstance(b, int) and b in SPLIT_AT:
                    whole, high, low = PARTS[SPLIT_AT.index(b)]
                    ffn_weights.wait(eng, N_FFN)
                    weights_h.done(eng.activation(high, whole, ACT.Copy))

            def context(b, q):
                c["PV"].wait(eng, 4 * b + 4)
                c["OT"].wait(eng, b)
                c["U"].done(eng.activation(uT[:, :, :], u_b[:, :].rearrange("p (g t) -> p g t", g=GROUPS),
                                           ACT.Copy))

            def heads(b, q):
                c["onT"].wait(eng, b + 1)
                c["O"].wait(eng, b)
                c["onT_e"].done(eng.activation(onT[:, :], m_c[:, 0:P], ACT.Copy))

            def normed(b, q):
                c["xn2T"].wait(eng, b + 1)
                c["logits"].wait(eng, b)
                c["xn2T_e"].done(eng.activation(xn2T[:, :], m_c[:, 0:P], ACT.Copy))

            def ranks(b, q):
                c["pos"].wait(eng, b + 1)
                c["xn2T"].wait(eng, upto_b(b + 3))
                c["row_of"].wait(eng, b)
                c["pos_e"].done(eng.activation(pos[:, :, :],
                                               m_c[:, P:P + 2 * E].rearrange("p (a e) -> p a e", a=2), ACT.Copy))

            def router(b, q):
                h = q % 2
                c["lmax"].wait(eng, b + 1)
                c["gate_w"].wait(eng, b - 1)
                c["ex"].done(eng.activation(ex[:, h, :], m_a[:, 0:E], ACT.Exp, bias=lmax[:, 0:1],
                                            accum_out=esum[:, h:h + 1]))

            batches(eng, [(g, exps(g)) for g in range(4)] +
                    [(20, router), (-12, normalise(1, lambda q: x_s[:, q, :], "xn", 2, xn)),
                     (15, normalise(2, lambda q: x2s[:, q % 2, :], "xn2", 4, xn2)),
                     (-7, queries), (9, heads), (-10, inputs), (-6, values), (16, normed), (24, ranks)] +
                    [(g + 1, probs(g)) for g in range(4)] + [(5, context), (13, late_keep), (2, high_parts)])

            def tokens_high(t, q):
                f["xT"].wait(eng, t + 1)
                f["h"].wait(eng, t - 3)
                f["xT_h"].done(eng.activation(xsT_h[:, q, :], xT_b[:, 0:P], ACT.Copy))

            def silu(t, q):
                h = q % 2
                f["h"].wait(eng, t + 1)
                f["hid"].wait(eng, t - 1)
                f["act"].done(eng.activation(act[:, h, :], h1_b[h][:, 0:HID], ACT.Silu))

            def result(t, q):
                f["y"].wait(eng, t + 1)
                tile_out[q].reusable(eng, t, q)
                f["y_e"].done(eng.activation(y_s[:, q, :], y_b[:, 0:D], ACT.Copy))

            tiles(eng, [(0, silu), (-2, tokens_high), (2, result)])

            def store(n, q):
                total.wait(eng, n + 1)
                dst = out.rearrange("b s d -> s b d")[:, bass.ds(n * LG, LG), :]
                stored[q].done(eng.dma_start(dst, tot[:, q, :, :]))

            with eng.Fori(0, B // LG // YB) as r:
                for q in range(YB):
                    store(r * YB + q, q)
            for q in range(YB):
                stored[q].wait(eng, B // LG // YB)

        @block.tensor
        def _(eng):
            ready.wait(eng, 3)
            bo_p.done(eng.matmul(m_c[:, 0:D], bv_s[:, 0:1].broadcast_to((P, P)), wo_s[:, :],
                                 start=True, stop=True))
            bo_ready.wait(eng, 1)

            def keep_clock_up(n):
                for _ in range(n):
                    eng.matmul(m_c[:, :], ones[:, :], ones[:, 0:1].broadcast_to((P, 512)), start=True, stop=True)

            def inputs(b, q):
                h = q % 2
                c["xn"].wait(eng, b + 1)
                c["qT_l"].wait(eng, b)
                eng.transpose(m_a[:, 0:D], xn[:, h, :], ident[:, :])
                c["ln1T"].done(eng.transpose(m_a[:, D:D + K], c_s[0:K, q, :], ident[0:K, 0:K]))

            def project(b, q):
                c["ln1T_e"].wait(eng, b + 1)
                c["ex"].wait(eng, b - 6)
                c["v"].wait(eng, b)
                c["on"].wait(eng, b - 3)
                eng.matmul(m_a[:, 0:P], wq_s[:, :], xcT[:, 0:D], start=True, stop=True)
                eng.matmul(m_b[:, 0:K], wk_s[:, :], xcT[:, D:D + K], start=True, stop=True)
                c["proj"].done(eng.matmul(m_b[0:K, P:2 * P], xcT[:, D:D + K], wv_s[:, :], start=True, stop=True))

            def scores(g):
                def run(b, q):
                    n, h = 4 * b + g, g % 2
                    r = slice(32 * g, 32 * g + 32)
                    if g == 0:
                        if isinstance(b, int) and b == 0:
                            keep_clock_up(16)
                        c["qT_l"].wait(eng, b + 1)
                        c["kz_h"].wait(eng, b + 1)
                        c["kz_l"].wait(eng, b + 1)
                    scores_out(eng, b, g)
                    c["S"].done(three_passes(
                        eng, score_b[h][:, 0:4 * K], (qT_h[r, q, :], qT_l[r, q, :]),
                        [kz[r, q % 2, :, :].rearrange("p j k -> p (j k)") for kz in (kz_h, kz_l)],
                        tile_position=(32 * g, 0)))
                return run

            def turn(g):
                def run(b, q):
                    n, h = 4 * b + g, g % 2
                    c["exp"].wait(eng, n + 1)
                    c["PT_e"].wait(eng, n - 1)
                    for j in range(4):
                        ins = eng.transpose(prT_b[h][0:K, j * P:j * P + P], prob[:, g, j, :], ident[:, :])
                    c["PT"].done(ins)
                return run

            def mix(g):
                def run(b, q):
                    n, h = 4 * b + g, g % 2
                    c["PT_e"].wait(eng, n + 1)
                    if g == 0:
                        c["v"].wait(eng, b + 1)
                        c["U"].wait(eng, b)
                    for j in range(4):
                        ins = eng.matmul(u_b[32 * j:32 * j + DH + 1, g * P:g * P + P],
                                         v1[0:K, q, 4 * g + j, :], pT[0:K, g, j, :],
                                         start=True, stop=True, tile_position=(0, 32 * j))
                    c["PV"].done(ins)
                return run

            def back(b, q):
                c["U"].wait(eng, b + 1)
                c["kT_l"].wait(eng, upto_b(b + 4))
                c["v"].wait(eng, upto_b(b + 4))
                for g in range(GROUPS):
                    ins = eng.transpose(m_b[:, g * P:g * P + P], uT[:, g, :], ident[:, :])
                c["OT"].done(ins)

            def heads(b, q):
                c["on"].wait(eng, b + 1)
                c["xn2T_e"].wait(eng, b - 1)
                c["pos_e"].wait(eng, b - 3)
                c["x2"].wait(eng, b)
                c["onT"].done(eng.transpose(m_c[:, 0:P], on[:, :], ident[:, :]))

            def out_proj(b, q):
                c["onT_e"].wait(eng, b + 1)
                c["O"].done(eng.matmul(m_c[:, 0:D], onT[:, :], wo_s[:, :], start=True, stop=True))

            def normed(b, q):
                c["xn2"].wait(eng, b + 1)
                c["x2"].wait(eng, upto_b(b + 2))
                c["xn2T_e"].wait(eng, b)
                c["pos_e"].wait(eng, b - 2)
                c["xn2T"].done(eng.transpose(m_c[:, 0:P], xn2[:, q, :], ident[:, :]))

            def router(b, q):
                c["xn2T_e"].wait(eng, b + 1)
                c["ln1T_e"].wait(eng, upto_b(b + 8))
                c["ex"].wait(eng, b)
                c["logits"].done(eng.matmul(m_a[:, 0:E], xn2T[:, :], gate_s[:, :], start=True, stop=True))

            def ranks(b, q):
                c["chosen"].wait(eng, b + 1)
                c["x2"].wait(eng, upto_b(b + 4))
                c["xn2T_e"].wait(eng, upto_b(b + 2))
                c["pos_e"].wait(eng, b)
                for n, over in enumerate((before, ones)):
                    for k in range(2):
                        ins = eng.matmul(m_c[:, P + n * E:P + n * E + E], over[:, :], chosen[:, q % 2, k, :],
                                         start=(k == 0), stop=(k == 1))
                c["pos"].done(ins)

            batches(eng, [(g - 1, scores(g)) for g in range(4)] +
                    [(-7, project), (10, out_proj), (-10, inputs), (7, back), (9, heads), (24, ranks),
                     (16, normed), (19, router)] +
                    [(g + 1, turn(g)) for g in range(4)] + [(g + 2, mix(g)) for g in range(4)])

            ended.wait(eng, 1)
            keep_clock_up(30)
            table.wait(eng, 4)
            ffn_weights.wait(eng, N_FFN)
            weights_l.wait(eng, len(PARTS))
            old = [eng.alloc_register(f"old_expert{n}") for n in range(4)]
            now = [eng.alloc_register(f"expert{n}") for n in range(4)]

            def expert(q, group):
                own = eng.alloc_register(f"tile_expert{next(names)}")
                eng.reg_mov(own, group[q])
                return bass.RuntimeValue.of_register_unchecked(own).with_bounds(min_val=0, max_val=E - 1)

            def tokens(t, q):
                tile_in[q].landed(eng, t, q)
                f["xT_l"].wait(eng, t)
                f["xT"].done(eng.transpose(xT_b[:, 0:P], xs[:, q, 0:D], ident[:, :]))

            def up(t, q):
                h = q % 2
                f["xT_l"].wait(eng, t + 1)
                f["hid"].wait(eng, t - 1)
                e = expert(q, now)
                tok = xsT_h[:, q, :], xsT_l[:, q, :]
                cols = bass.ds(e * HID, HID)
                three_passes(eng, h1_b[h][:, 0:HID], tok, (w1_h[:, cols], w1_l[:, cols]))
                f["h"].done(three_passes(eng, h3_b[h][:, 0:HID], tok, (w3_h[:, cols], w3_l[:, cols])))

            def turn_hidden(t, q):
                h = q % 2
                f["hid"].wait(eng, t + 1)
                f["hT_e"].wait(eng, t - 1)
                for k in range(HC):
                    ins = eng.transpose(hT_b[h][0:CHUNK[k], k * P:k * P + P],
                                        hid[:, h, k * P:k * P + CHUNK[k]], ident[:, :])
                f["hT"].done(ins)

            def down(t, q):
                h = q % 2
                f["hT_e"].wait(eng, t + 1)
                f["y_e"].wait(eng, t)
                e = expert(q, now if q < 2 else old)
                for k in range(HC):
                    ins = eng.matmul(y_b[:, 0:D], hidT[0:CHUNK[k], h, k, :],
                                     w2_s[0:CHUNK[k], k, bass.ds(e * D, D)],
                                     start=(k == 0), stop=(k == HC - 1))
                f["y"].done(ins)

            def experts(t, q):
                if q == 0:
                    eng.load(old + now, t_exp[0:1, bass.ds(t, 8)])

            tiles(eng, [(0, experts), (0, up), (1, turn_hidden), (-2, tokens), (2, down)])


def kernel(**inputs):
    import numpy as np
    import concourse.bacc as bacc
    from concourse.bass_utils import run_bass_kernel_spmd

    p = "L0_xattn_"
    laid = {
        "x": inputs["x"], "ctx_in": inputs["ctx_1024"],
        "wqT": inputs[p + "wq"].T, "bq": inputs[p + "bq"], "wkT": inputs[p + "wk"].T, "bk": inputs[p + "bk"],
        "wvT": inputs[p + "wv"].T, "bv": inputs[p + "bv"], "woT": inputs[p + "wo"].T, "bo": inputs[p + "bo"],
        "gateT": inputs["L0_ffn_gate_w"].T, "ebias": inputs["L0_ffn_expert_bias"],
        "w1": inputs["L0_ffn_w1"], "w2": inputs["L0_ffn_w2"], "w3": inputs["L0_ffn_w3"],
    }
    nc = bacc.Bacc("TRN2", target_bir_lowering=False, num_devices=1)
    arrays, args = {}, {}
    for name, value in laid.items():
        a = np.ascontiguousarray(value)
        arrays[f"in_{name}"] = a
        args[name] = nc.dram_tensor(f"in_{name}", a.shape, mybir.dt.from_np(a.dtype), kind="ExternalInput").ap()
    out = nc.dram_tensor("out_0", laid["x"].shape, F32, kind="ExternalOutput").ap()
    build(nc, out=out, **args)
    r = run_bass_kernel_spmd(nc, [arrays], core_ids=[0])
    return r.results[0]["out_0"]
```
